# Optimizing a Trainium2 kernel written in Bass

```python
import numpy as np
import jax
import jax.numpy as jnp

def _softmax(x, axis=-1):
    return jax.nn.softmax(x, axis=axis)

def _gelu(x):
    return jax.nn.gelu(x, approximate=True)

def _silu(x):
    return jax.nn.silu(x)

def _sigmoid(x):
    return jax.nn.sigmoid(x)

def _layernorm(x, axis=-1, eps=1e-05):
    m = jnp.mean(x, axis=axis, keepdims=True)
    v = jnp.var(x, axis=axis, keepdims=True)
    return (x - m) / jnp.sqrt(v + eps)

def _scatter_add(tgt, idx, src, axis=0):
    return tgt.at[idx].add(src)

def _segment_sum(src, seg, n):
    return jax.ops.segment_sum(src, seg, n)
kernel_name = 'mk_adj_ffn_d2_adj_r2_2978a7'

def setup_inputs(seed: int=0):
    np.random.seed(seed)
    _w = jnp.asarray

    def _rec_inputs():
        import jax
        import jax.numpy as jnp
        _gk = jax.random.key(seed)
        x = -0.000929 + 1 * jax.random.normal(jax.random.fold_in(_gk, 1), (16, 512, 128), jnp.float32)
        _a = jax.random.bernoulli(jax.random.fold_in(_gk, 2), 0.015625, (16, 512, 512))
        _a = jnp.logical_or(_a, jnp.eye(512, dtype=bool))
        _af = _a.astype(jnp.float32)
        adj = _af
        return (x, adj)
    x, adj = _rec_inputs()

    def _L0_gnn_setup():
        import jax, jax.numpy as jnp
        import numpy as np
        B, N = (1, 2048)
        D_IN, D_OUT, H = (128, 128, 8)
        HD = D_OUT // H
        NEG = -9000000000000000.0

        def _xavier(key, shape):
            lim = np.sqrt(6.0 / (shape[0] + shape[1])).astype(np.float32)
            return jax.random.uniform(key, shape, jnp.float32, -lim, lim)
        key = jax.random.key(seed)
        ks = jax.random.split(key, 8)
        x = jax.random.normal(ks[0], (B, N, D_IN), jnp.float32)
        adj = (jax.random.uniform(ks[1], (B, N, N)) < 0.05).astype(jnp.float32)
        idx = jnp.arange(N)
        adj = adj.at[:, idx, idx].set(1.0)
        Wq = _xavier(ks[2], (D_IN, D_OUT))
        bq = jnp.zeros((D_OUT,), jnp.float32)
        Wk = _xavier(ks[3], (D_IN, D_OUT))
        bk = jnp.zeros((D_OUT,), jnp.float32)
        Wv = _xavier(ks[4], (D_IN, D_OUT))
        bv = jnp.zeros((D_OUT,), jnp.float32)
        Wo = _xavier(ks[5], (D_OUT, D_OUT))
        bo = jnp.zeros((D_OUT,), jnp.float32)
        return dict(x=x, adj=adj, Wq=Wq, bq=bq, Wk=Wk, bk=bk, Wv=Wv, bv=bv, Wo=Wo, bo=bo)
    _L0_gnn_all = _L0_gnn_setup()
    _L0_gnn_in = {k: v for k, v in _L0_gnn_all.items() if k in ('Wq', 'bq', 'Wk', 'bk', 'Wv', 'bv', 'Wo', 'bo')}
    del _L0_gnn_all

    def _L0_ffn_setup():
        import jax, jax.numpy as jnp
        import numpy as np
        DIM = 128
        HEADS = 8
        NUM_KEYS = 128
        NUM_KV = NUM_KEYS ** 2
        PK_TOPK = 16
        FINAL_TOPK = 16
        DIM_KEY = DIM // 2
        P = 2

        def _pk(x, Wq_pk, pk_keys):
            b, n, _ = x.shape
            q = (x @ Wq_pk).reshape(b, n, P, HEADS, DIM_KEY).transpose(2, 0, 1, 3, 4)
            sim = jnp.einsum('pbnhd,pkhd->pbnhk', q, pk_keys)
            scores, idx = jax.lax.top_k(sim, PK_TOPK)
            idx0 = idx[0]
            idx1 = idx[1] * NUM_KEYS
            index = (idx0[..., :, None] + idx1[..., None, :]).reshape(b, n, HEADS, PK_TOPK * PK_TOPK)
            score = (scores[0][..., :, None] + scores[1][..., None, :]).reshape(b, n, HEADS, PK_TOPK * PK_TOPK)
            final_scores, pk_idx = jax.lax.top_k(score, FINAL_TOPK)
            final_indices = jnp.take_along_axis(index, pk_idx, axis=-1)
            final_scores = jax.nn.softmax(final_scores, axis=-1)
            return (final_scores, final_indices)
        key = jax.random.key(seed)
        ks = jax.random.split(key, 7)
        b, n = (2, 512)
        std = 0.02
        x = jax.random.normal(ks[0], (b, n, DIM), dtype=jnp.float32)
        Wq_pk = jax.random.normal(ks[1], (DIM, P * HEADS * DIM_KEY), dtype=jnp.float32) * std
        pk_keys = jax.random.normal(ks[2], (P, NUM_KEYS, HEADS, DIM_KEY), dtype=jnp.float32) * std
        Wq = jax.random.normal(ks[3], (DIM, HEADS * DIM), dtype=jnp.float32) * std
        keys_table = jax.random.normal(ks[4], (NUM_KV * HEADS, DIM), dtype=jnp.float32) * std
        values_table = jax.random.normal(ks[5], (NUM_KV * HEADS, DIM), dtype=jnp.float32) * std
        Wo = jax.random.normal(ks[6], (DIM * HEADS, DIM), dtype=jnp.float32) * std
        return {'x': x, 'Wq_pk': Wq_pk, 'pk_keys': pk_keys, 'Wq': Wq, 'keys_table': keys_table, 'values_table': values_table, 'Wo': Wo}
    _L0_ffn_all = _L0_ffn_setup()
    _L0_ffn_in = {k: v for k, v in _L0_ffn_all.items() if k in ('Wq_pk', 'pk_keys', 'Wq', 'keys_table', 'values_table', 'Wo')}
    del _L0_ffn_all

    def _L1_gnn_setup():
        import math
        import jax, jax.numpy as jnp
        import numpy as np
        B, N, D, H = (32, 256, 128, 8)
        HD = D // H
        key = jax.random.key(seed)
        ks = jax.random.split(key, 9)
        h = jax.random.normal(ks[0], (B, N, D), dtype=jnp.float32)
        edge = jax.random.normal(ks[1], (B, N, N), dtype=jnp.float32)
        adj = jax.random.uniform(ks[2], (B, N, N)) < 0.5
        adj_mask = adj | jnp.eye(N, dtype=bool)[None]
        s = 1.0 / math.sqrt(D)
        W_q = jax.random.normal(ks[3], (D, D), dtype=jnp.float32) * s
        W_k = jax.random.normal(ks[4], (D, D), dtype=jnp.float32) * s
        W_v = jax.random.normal(ks[5], (D, D), dtype=jnp.float32) * s
        W_e = jax.random.normal(ks[6], (H, 1), dtype=jnp.float32)
        W_o = jax.random.normal(ks[7], (D, D), dtype=jnp.float32) * s
        return {'h': h, 'edge': edge, 'adj_mask': adj_mask, 'W_q': W_q, 'W_k': W_k, 'W_v': W_v, 'W_e': W_e, 'W_o': W_o}
    _L1_gnn_all = _L1_gnn_setup()
    _L1_gnn_in = {k: v for k, v in _L1_gnn_all.items() if k in ('W_q', 'W_k', 'W_v', 'W_e', 'W_o')}
    del _L1_gnn_all

    def _L1_ffn_setup():
        import jax, jax.numpy as jnp
        import numpy as np
        C = 128
        EPS = 1e-05
        N_ITERS = 30

        def _layernorm(x, w, bias):
            mu = jnp.mean(x, axis=-1, keepdims=True)
            var = jnp.mean(jnp.square(x - mu), axis=-1, keepdims=True)
            return (x - mu) * jax.lax.rsqrt(var + EPS) * w + bias
        key = jax.random.key(seed)
        kx, kw, kb, klw, klb = jax.random.split(key, 5)
        x = jax.random.normal(kx, (8, 1024, C), dtype=jnp.float32)
        bound = 1.0 / np.sqrt(C)
        W = jax.random.uniform(kw, (C, C), minval=-bound, maxval=bound, dtype=jnp.float32)
        b = jax.random.uniform(kb, (C,), minval=-bound, maxval=bound, dtype=jnp.float32)
        ln_w = jnp.ones((C,), dtype=jnp.float32)
        ln_b = jnp.zeros((C,), dtype=jnp.float32)
        return {'x': x, 'ln_w': ln_w, 'ln_b': ln_b, 'W': W, 'b': b}
    _L1_ffn_all = _L1_ffn_setup()
    _L1_ffn_in = {k: v for k, v in _L1_ffn_all.items() if k in ('ln_w', 'ln_b', 'W', 'b')}
    del _L1_ffn_all
    return {'x': x, 'adj': adj, 'L0_gnn_Wq': _L0_gnn_in['Wq'], 'L0_gnn_bq': _L0_gnn_in['bq'], 'L0_gnn_Wk': _L0_gnn_in['Wk'], 'L0_gnn_bk': _L0_gnn_in['bk'], 'L0_gnn_Wv': _L0_gnn_in['Wv'], 'L0_gnn_bv': _L0_gnn_in['bv'], 'L0_gnn_Wo': _L0_gnn_in['Wo'], 'L0_gnn_bo': _L0_gnn_in['bo'], 'L0_ffn_Wq_pk': _L0_ffn_in['Wq_pk'], 'L0_ffn_pk_keys': _L0_ffn_in['pk_keys'], 'L0_ffn_Wq': _L0_ffn_in['Wq'], 'L0_ffn_keys_table': _L0_ffn_in['keys_table'], 'L0_ffn_values_table': _L0_ffn_in['values_table'], 'L0_ffn_Wo': _L0_ffn_in['Wo'], 'L1_gnn_W_q': _L1_gnn_in['W_q'], 'L1_gnn_W_k': _L1_gnn_in['W_k'], 'L1_gnn_W_v': _L1_gnn_in['W_v'], 'L1_gnn_W_e': _L1_gnn_in['W_e'], 'L1_gnn_W_o': _L1_gnn_in['W_o'], 'L1_ffn_ln_w': _L1_ffn_in['ln_w'], 'L1_ffn_ln_b': _L1_ffn_in['ln_b'], 'L1_ffn_W': _L1_ffn_in['W'], 'L1_ffn_b': _L1_ffn_in['b']}

def reference(x, adj, L0_gnn_Wq, L0_gnn_bq, L0_gnn_Wk, L0_gnn_bk, L0_gnn_Wv, L0_gnn_bv, L0_gnn_Wo, L0_gnn_bo, L0_ffn_Wq_pk, L0_ffn_pk_keys, L0_ffn_Wq, L0_ffn_keys_table, L0_ffn_values_table, L0_ffn_Wo, L1_gnn_W_q, L1_gnn_W_k, L1_gnn_W_v, L1_gnn_W_e, L1_gnn_W_o, L1_ffn_ln_w, L1_ffn_ln_b, L1_ffn_W, L1_ffn_b):
    import jax
    import jax.numpy as jnp

    def _L0_gnn_ref(x, adj, Wq, bq, Wk, bk, Wv, bv, Wo, bo):
        import jax, jax.numpy as jnp
        import numpy as np
        B, N = (1, 2048)
        D_IN, D_OUT, H = (128, 128, 8)
        HD = D_OUT // H
        NEG = -9000000000000000.0

        def _xavier(key, shape):
            lim = np.sqrt(6.0 / (shape[0] + shape[1])).astype(np.float32)
            return jax.random.uniform(key, shape, jnp.float32, -lim, lim)
        b, n, _ = x.shape

        def split_heads(t):
            return t.reshape(b, n, H, HD).transpose(0, 2, 1, 3)
        q = split_heads(x @ Wq + bq)
        k = split_heads(x @ Wk + bk)
        v = split_heads(x @ Wv + bv)
        scores = jnp.einsum('bhqd,bhkd->bhqk', q, k) / np.float32(np.sqrt(HD))
        scores = jnp.where(adj[:, None, :, :] > 0, scores, jnp.float32(NEG))
        attn = jax.nn.softmax(scores, axis=-1)
        out = jnp.einsum('bhqk,bhkd->bhqd', attn, v)
        out = out.transpose(0, 2, 1, 3).reshape(b, n, D_OUT)
        return out @ Wo + bo

    def _L0_ffn_ref(x, Wq_pk, pk_keys, Wq, keys_table, values_table, Wo):
        import jax, jax.numpy as jnp
        import numpy as np
        DIM = 128
        HEADS = 8
        NUM_KEYS = 128
        NUM_KV = NUM_KEYS ** 2
        PK_TOPK = 16
        FINAL_TOPK = 16
        DIM_KEY = DIM // 2
        P = 2

        def _pk(x, Wq_pk, pk_keys):
            b, n, _ = x.shape
            q = (x @ Wq_pk).reshape(b, n, P, HEADS, DIM_KEY).transpose(2, 0, 1, 3, 4)
            sim = jnp.einsum('pbnhd,pkhd->pbnhk', q, pk_keys)
            scores, idx = jax.lax.top_k(sim, PK_TOPK)
            idx0 = idx[0]
            idx1 = idx[1] * NUM_KEYS
            index = (idx0[..., :, None] + idx1[..., None, :]).reshape(b, n, HEADS, PK_TOPK * PK_TOPK)
            score = (scores[0][..., :, None] + scores[1][..., None, :]).reshape(b, n, HEADS, PK_TOPK * PK_TOPK)
            final_scores, pk_idx = jax.lax.top_k(score, FINAL_TOPK)
            final_indices = jnp.take_along_axis(index, pk_idx, axis=-1)
            final_scores = jax.nn.softmax(final_scores, axis=-1)
            return (final_scores, final_indices)
        b, n, d = x.shape
        q = (x @ Wq).reshape(b, n, HEADS, DIM) * DIM ** (-0.5)
        kv_scores, indices = _pk(x, Wq_pk, pk_keys)
        offsets = jnp.arange(HEADS, dtype=indices.dtype) * NUM_KV
        ind = indices + offsets[None, None, :, None]
        k = jnp.einsum('bnhk,bnhkd->bnhd', kv_scores, keys_table[ind])
        v = jnp.einsum('bnhk,bnhkd->bnhd', kv_scores, values_table[ind])
        sim = jnp.einsum('bihd,bjhd->bhij', q, k)
        neg = -jnp.finfo(sim.dtype).max
        causal = jnp.tril(jnp.ones((n, n), dtype=bool))
        sim = jnp.where(causal, sim, neg)
        attn = jax.nn.softmax(sim, axis=-1)
        out = jnp.einsum('bhij,bjhd->bhid', attn, v)
        out = out.transpose(0, 2, 1, 3).reshape(b, n, HEADS * DIM)
        return out @ Wo

    def _L1_gnn_ref(h, edge, adj_mask, W_q, W_k, W_v, W_e, W_o):
        import math
        import jax, jax.numpy as jnp
        import numpy as np
        B, N, D, H = (32, 256, 128, 8)
        HD = D // H
        b, n, _ = h.shape
        q = (h @ W_q.T).reshape(b, n, H, HD).transpose(0, 2, 1, 3)
        k = (h @ W_k.T).reshape(b, n, H, HD).transpose(0, 2, 1, 3)
        v = (h @ W_v.T).reshape(b, n, H, HD).transpose(0, 2, 1, 3)
        edge_bias = jnp.einsum('bij,h->bhij', edge, W_e[:, 0])
        scores = jnp.einsum('bhid,bhjd->bhij', q, k) / math.sqrt(HD) + edge_bias
        scores = jnp.where(adj_mask[:, None], scores, -jnp.inf)
        attn = jax.nn.softmax(scores, axis=-1)
        out = jnp.einsum('bhij,bhjd->bhid', attn, v)
        out = out.transpose(0, 2, 1, 3).reshape(b, n, D)
        return out @ W_o.T

    def _L1_ffn_ref(x, ln_w, ln_b, W, b):
        import jax, jax.numpy as jnp
        import numpy as np
        C = 128
        EPS = 1e-05
        N_ITERS = 30

        def _layernorm(x, w, bias):
            mu = jnp.mean(x, axis=-1, keepdims=True)
            var = jnp.mean(jnp.square(x - mu), axis=-1, keepdims=True)
            return (x - mu) * jax.lax.rsqrt(var + EPS) * w + bias

        def step(h, _):
            h = h + 0.01 * jnp.tanh(h)
            h = h * jax.nn.sigmoid(h)
            h = _layernorm(h, ln_w, ln_b)
            h = jnp.einsum('bsc,dc->bsd', h, W) + b
            return (h, None)
        x, _ = jax.lax.scan(step, x, None, length=N_ITERS)
        return x
    x = x + _L0_gnn_ref(_layernorm(x, axis=-1), adj, L0_gnn_Wq, L0_gnn_bq, L0_gnn_Wk, L0_gnn_bk, L0_gnn_Wv, L0_gnn_bv, L0_gnn_Wo, L0_gnn_bo)
    x = x + _L0_ffn_ref(_layernorm(x, axis=-1), L0_ffn_Wq_pk, L0_ffn_pk_keys, L0_ffn_Wq, L0_ffn_keys_table, L0_ffn_values_table, L0_ffn_Wo)
    x = x + _L1_gnn_ref(_layernorm(x, axis=-1), adj, adj, L1_gnn_W_q, L1_gnn_W_k, L1_gnn_W_v, L1_gnn_W_e, L1_gnn_W_o)
    x = x + _L1_ffn_ref(_layernorm(x, axis=-1), L1_ffn_ln_w, L1_ffn_ln_b, L1_ffn_W, L1_ffn_b)
    return x

_drawn_inputs = setup_inputs


def setup_inputs(seed=0):
    import zlib

    import numpy as np

    out = dict(_drawn_inputs(seed))
    spreads = {'L0_gnn_bq': (0.0, 0.1),
     'L0_gnn_bk': (0.0, 2.0),
     'L0_gnn_bv': (0.0, 0.1),
     'L0_gnn_bo': (0.0, 0.1),
     'L1_ffn_ln_w': (1.0, 0.2),
     'L1_ffn_ln_b': (0.0, 0.1)}
    factors = {'L0_ffn_Wq_pk': 8.0,
     'L0_ffn_pk_keys': 8.0,
     'L0_ffn_Wq': 64.0,
     'L0_ffn_keys_table': 64.0,
     'L0_ffn_values_table': 8.0,
     'L0_ffn_Wo': 8.0,
     'L1_gnn_W_e': 64.0}
    for name, (base, spread) in spreads.items():
        noise = np.random.default_rng([zlib.crc32(name.encode()), seed]).standard_normal(out[name].shape)
        drawn = base * np.exp(spread * noise) if base else spread * noise
        out[name] = jnp.asarray(drawn.astype(out[name].dtype))
    for name, factor in factors.items():
        out[name] = (out[name] * factor).astype(out[name].dtype)
    return out
```

```python
import numpy as np
import concourse.bass as bass
from concourse import mybir
from contextlib import ExitStack

P = 128
NB, S, D = 16, 512, 128
TILES = S // P
H, HD = 8, 16
NKEYS, DK, TOPK = 128, 64, 16
NKV = NKEYS * NKEYS
ITERS = 30
SLOTS = TILES * H
GROUPS = ((0, 1, 16), (1, 1, 8), (2, 2, 5), (4, 4, 3), (8, 8, 1))
NC = sum(r * c for _, r, c in GROUPS)
LAG = {"A": 0, "T": 1, "C": 2, "B": 3, "F": 4}
NEG0 = -9.0e15
NEG1 = -1.0e37
LOW = -3.0e38
EPS = 1e-5
NCONST = 9 + H + NC


def active(stage, period):
    return 0 <= period - 1 - LAG[stage] < NB


def build(nc, a, out):
    f32, bf16, u32, i32 = mybir.dt.float32, mybir.dt.bfloat16, mybir.dt.uint32, mybir.dt.int32
    ALU = mybir.AluOpType
    ACT = mybir.ActivationFunctionType
    AX = mybir.AxisListType.X
    LAST = NB + 4

    ctx = ExitStack()
    with ctx:
        x, adj = a["x"], a["adj"]

        def sb(name, shape, dt=f32):
            return ctx.enter_context(nc.sbuf_tensor(name, shape, dt))

        def pb(name, shape, dt=f32):
            return ctx.enter_context(nc.psum_tensor(name, shape, dt))

        def sem(name):
            return ctx.enter_context(nc.semaphore(name))

        starts = []

        def slot_sem(name, stage):
            s = sem(name)
            starts.append((s, SLOTS * (1 + LAG[stage])))
            return s

        def period_sem(name, first):
            s = sem(name)
            if first > 1:
                starts.append((s, first - 1))
            return s

        ident = sb("ident", [P, P])
        identh = sb("identh", [P, P], bf16)
        causal = sb("causal", [P, P], bf16)
        hmask = sb("hmask", [P, H])
        hoff = sb("hoff", [P, H])
        iota = sb("iota", [P, NC])
        we = sb("we", [P, H])
        w0q, w0k, w0v, w0o = (sb(n, [P, P]) for n in ("w0q", "w0k", "w0v", "w0o"))
        w1q, w1k, w1v, w1o = (sb(n, [P, P]) for n in ("w1q", "w1k", "w1v", "w1o"))
        b0q, b0k = sb("b0q", [P, 1]), sb("b0k", [P, 1])
        b0v, b0o = sb("b0v", [P, P]), sb("b0o", [P, P])
        simw = sb("simw", [P, H, 2, NKEYS])
        wcq = sb("wcq", [P, H * D])
        wco = sb("wco", [P, H, D])
        wf, bf = sb("wf", [P, P]), sb("bf", [P, P])
        lnw, lnb = sb("lnw", [P, 1]), sb("lnb", [P, 1])

        xin, x0, xa = sb("xin", [P, TILES, D]), sb("x0", [P, TILES, D]), sb("xa", [P, TILES, D])
        xg, xf = sb("xg", [P, TILES, D]), sb("xf", [P, TILES, D])
        xc = sb("xc", [P, TILES, D])
        qT = [sb(f"qT{g}", [P, S]) for g in range(2)]
        kT = [sb(f"kT{g}", [P, S]) for g in range(2)]
        vv = [sb(f"vv{g}", [P, TILES, D]) for g in range(2)]
        oo = [sb(f"oo{g}", [P, TILES, D]) for g in range(2)]
        adjt = [[sb(f"adj{g}{i}", [P, S]) for i in range(2)] for g in range(2)]
        maskt = [[sb(f"mask{g}{i}", [P, S], bf16) for i in range(2)] for g in range(2)]
        qz = [sb(f"qz{g}", [P, P]) for g in range(2)]
        pr = [sb(f"pr{g}", [P, S]) for g in range(3)]
        prT = [sb(f"prT{g}", [P, S]) for g in range(3)]
        nm = [sb(f"nm{g}", [P, 1]) for g in range(3)]
        rs = [sb(f"rs{g}", [P, 1]) for g in range(3)]
        rr = [sb(f"rr{g}", [P, 1]) for g in range(3)]

        xtT, xcT = sb("xtT", [P, S]), sb("xcT", [P, S])
        top = sb("top", [P, 2, TOPK])
        topi = sb("topi", [P, 2, TOPK], u32)
        cand, candr, candi = sb("cand", [P, NC]), sb("candr", [P, NC]), sb("candi", [P, NC])
        fin = sb("fin", [P, TOPK])
        pos = sb("pos", [P, TOPK], u32)
        hit = sb("hit", [P, TOPK, NC])
        rest = hit[:].rearrange("p j c -> p (j c)")[:, 0:2 * NKEYS].rearrange("p (a k) -> p a k", a=2)
        rowf = sb("rowf", [P, TOPK])
        negm, tsum, trec = sb("negm", [P, 1]), sb("tsum", [P, 1]), sb("trec", [P, 1])
        ew = sb("ew", [P, TOPK])
        row = [sb(f"row{i}", [P, TOPK], u32) for i in range(2)]
        wt = [sb(f"wt{i}", [P, TOPK]) for i in range(2)]
        G = [sb(f"G{i}", [P, TOPK, 2 * D]) for i in range(2)]
        dg = [sb(f"dg{i}", [P, TOPK, P]) for i in range(2)]
        KT = sb("KT", [P, 2 * SLOTS * P])
        VV = sb("VV", [P, 2 * SLOTS * P])

        wqs, qs, ocT = sb("wqs", [P, P]), sb("qs", [P, P]), sb("ocT", [P, P])
        oc = qs

        hh, h1, sg = sb("hh", [P, TILES, D]), sb("h1", [P, TILES, D]), sb("sg", [P, TILES, D])
        hT = sb("hT", [P, S])
        avg, wft = hh[:, 0, :], sg[:, 0, :]
        stats, mv = sb("stats", [P, TILES, 6]), sb("mv", [P, TILES, 2])
        va, ya, yb, yc = (sb(n, [P, TILES]) for n in ("va", "ya", "yb", "yc"))
        xn, oT = h1, hT
        lst, lmv = stats, mv

        bank = [pb(f"bank{i}", [P, 512]) for i in range(8)]
        SC = bank[0:3]
        psq = psC = psCT = SC[2][:, 0:128]
        psK = [b[:, 0:128] for b in (bank[3], bank[6])]
        psV = [b[:, 128:256] for b in (bank[3], bank[6])]
        psS = bank[4][:, 0:256]
        psO = [bank[7][:, 0:HD], bank[7][:, HD:2 * HD]]
        psH = psY = bank[5]
        psw = bank[5][:, 0:128]

        GS = ("A", "B")
        ld_w = sem("weights_loaded")
        ld_x = sem("x_loaded")
        ld_adj = [[sem(f"adj{g}{i}_loaded") for i in range(2)] for g in GS]
        mask_ready = [sem(f"mask{g}_ready") for g in GS]
        stored = sem("out_stored")
        const_ready = sem("const_ready")
        prep_pe, prep_act, prep_dve = sem("prep_pe"), sem("prep_act"), sem("prep_dve")
        dchain = sem("vector_chain")
        turn = [sem("top_turn"), sem("gather_turn")]
        qz_ready = [slot_sem(f"qz{g}_ready", g) for g in GS]
        sc_ready = [slot_sem(f"scores{g}_ready", g) for g in ("A", "B", "C")]
        nm_ready = [slot_sem(f"negmax{g}_ready", g) for g in ("A", "B", "C")]
        pr_ready = [slot_sem(f"probs{g}_ready", g) for g in ("A", "B", "C")]
        pt_ready = [slot_sem(f"probsT{g}_ready", g) for g in ("A", "B", "C")]
        ptsb_ready = [slot_sem(f"probsTcopy{g}_ready", g) for g in ("A", "B", "C")]
        av_ready = [slot_sem(f"av{g}_ready", g) for g in ("A", "B", "C")]
        wqs_ready = slot_sem("wqs_ready", "C")
        q_ready = slot_sem("q_ready", "C")
        qs_ready = slot_sem("qs_ready", "C")
        rc_ready = slot_sem("rowsum_recip_ready", "C")
        oc_ready = slot_sem("oc_ready", "C")
        oct_ready = slot_sem("ocT_ready", "C")
        octsb_ready = slot_sem("ocTcopy_ready", "C")
        wo_ready = slot_sem("wo_ready", "C")
        sim_ready = slot_sem("sim_ready", "T")
        ng_ready = slot_sem("negtop_ready", "T")
        ew_ready = slot_sem("topexp_ready", "T")
        row_ready = slot_sem("rows_ready", "T")
        wt_ready = slot_sem("topweights_ready", "T")
        gathered = [sem(f"gathered{i}") for i in range(2)]
        gathered_last = [sem(f"gathered_last{i}") for i in range(2)]
        dg_ready = [sem(f"diag_half{i}_ready") for i in range(2)]
        sum_ready = sem("sums_ready")
        sumsb_ready = sem("sumcopy_ready")
        for q in (*dg_ready, sum_ready, sumsb_ready):
            starts.append((q, 2 * SLOTS + 2))
        th_ready = slot_sem("tanh_ready", "F")
        h1_ready = slot_sem("h1_ready", "F")
        sg_ready = slot_sem("tanh_half_ready", "F")
        h2_ready = slot_sem("h2_ready", "F")
        h2t_ready = slot_sem("h2T_ready", "F")
        h2tsb_ready = slot_sem("h2Tcopy_ready", "F")
        y_ready = slot_sem("y_ready", "F")
        f_ready = sem("h_ready")
        starts.append((f_ready, SLOTS * (1 + LAG["F"]) - 2))
        pe_done, act_done, dve_done = sem("pe_period"), sem("act_period"), sem("dve_period")
        g1_oT, g1_oTsb, g1_pr = (period_sem(f"bB_{n}", 5) for n in ("oT", "oTcopy", "proj"))
        c_xn, c_xT, c_xTsb, c_q, c_qsb = (period_sem(f"bC_{n}", 4) for n in ("xn", "xT", "xTcopy", "qkv", "qkvcopy"))
        t_cp = period_sem("bT_copy", 3)
        g0_oT, g0_oTsb, g0_pr, g0_xn, g0_xT, g0_xTsb = (
            period_sem(f"bA_{n}", 2) for n in ("oT", "oTcopy", "proj", "xn", "xT", "xTcopy"))
        i_xn, i_xT, i_xTsb, i_q, i_qsb = (period_sem(f"bI_{n}", 1) for n in ("xn", "xT", "xTcopy", "qkv", "qkvcopy"))
        i_v = period_sem("bI_v", 1)
        o_ready = period_sem("result_ready", 6)
        x_used = sem("xin_used")

        block = ctx.enter_context(nc.Block())

        def periods(eng, one):
            for p in range(1, 6):
                one(p, p)
            with eng.Fori(6, NB + 1) as p:
                one(p, 6)
            for p in range(NB + 1, LAST + 1):
                one(p, p)

        def slots(eng, p, like, slot):
            fl = {g for g in "ATCBF" if active(g, like)}
            for tile in range(TILES):
                w = active("T", like)
                wprev = active("T", like - 1)
                cuts = [(0, 2, w if tile else wprev), (2, 6, w), (6, 8, w)]
                for lo, hi, ws in cuts:
                    stages = set(fl)
                    if ws:
                        stages.add("W")
                    if tile == TILES - 1 and lo == 6:
                        stages.discard("F")
                    if not stages:
                        continue
                    if hi - lo > 2:
                        with eng.Fori(lo, hi, 2) as j:
                            for s in range(2):
                                slot(tile, s, j + s, p * SLOTS + tile * H + s + j, stages)
                    else:
                        for s in range(2):
                            slot(tile, s, lo + s, p * SLOTS + (tile * H + lo + s), stages)

        def snap(eng, v):
            return v if isinstance(v, int) else eng.snap(v)

        def across(v):
            return v.rearrange("(o n) -> o n", o=1).to_broadcast([P, v.shape[0]])

        def column(v):
            return v.rearrange("(p o) -> p o", o=1)

        pkq = G[0][0:DK, 0:8, :].rearrange("p a b -> p (a b)")
        pkk = G[1][0:DK, 0:8, :].rearrange("p a b -> p (a b)")
        LOADS = [(w0q[:], a["w0q"]), (w0k[:], a["w0k"]), (w0v[:], a["w0v"]), (w0o[:], a["w0o"]),
                 (w1q[:], a["w1q"]), (w1k[:], a["w1k"]), (w1v[:], a["w1v"]), (w1o[:], a["w1o"]),
                 (b0q[:], column(a["b0q"])), (b0k[:], column(a["b0k"])), (b0v[:], across(a["b0v"])),
                 (b0o[:], across(a["b0o"])), (we[:], across(a["we"])), (wcq[:], a["wcq"]),
                 (wco[:], a["wco"].rearrange("(h d) c -> d h c", d=D)), (wft, a["wft"]), (bf[:], across(a["bf"])),
                 (lnw[:], column(a["lnw"])), (lnb[:], column(a["lnb"])), (pkq, a["pkq"]), (pkk, a["pkk"])]

        @block.sync
        def _(sp):
            for q, v in starts:
                sp.sem_inc(q, v)
            for i, (dst, src) in enumerate(LOADS):
                sp.dma_start(dst, src).then_inc(ld_w, 16)

            def one(p, like):
                if active("A", like):
                    if like > 1:
                        sp.wait_ge(x_used, p - 1)
                    sp.dma_start(xin[:], x[bass.ds(p - 1, 1)].rearrange("b (t p) c -> p (b t) c", p=P)).then_inc(ld_x, 16)
                for t in range(TILES):
                    for g in range(2):
                        if active(GS[g], like):
                            first = 1 + LAG[GS[g]]
                            if t >= 2 or like > first:
                                if g == 0:
                                    sp.wait_ge(mask_ready[0], (p - first) * TILES + t - 1)
                                else:
                                    sp.wait_ge(nm_ready[1], p * SLOTS + (t - 1) * H)
                            sp.dma_start(adjt[g][t % 2][:], adj[bass.ds(p - first, 1), t * P:(t + 1) * P, :]
                                         .rearrange("b p k -> p (b k)")).then_inc(ld_adj[g][t % 2], 16)
                    if t == 0 and active("F", like - 1):
                        sp.wait_ge(o_ready, p)
                        sp.dma_start(out[bass.ds(p - 6, 1)].rearrange("b (t p) c -> p (b t) c", p=P), xf[:]).then_inc(stored, 16)
            periods(sp, one)
            sp.wait_ge(o_ready, LAST + 1)
            sp.dma_start(out[NB - 1].rearrange("(t p) c -> p t c", p=P), xf[:]).then_inc(stored, 16)
            sp.wait_ge(stored, 16 * NB)

        @block.gpsimd
        def _(gp):
            done = [0]

            def link(ins):
                done[0] += 1
                ins.then_inc(const_ready, 1)
                gp.wait_ge(const_ready, done[0])

            link(gp.memset(ident[:], 0.0))
            link(gp.affine_select(out=ident[:], in_=ident[:], compare_op=ALU.not_equal, fill=1.0, base=0,
                                  pattern=[[-1, P]], channel_multiplier=1))
            link(gp.tensor_copy(identh[:], ident[:]))
            link(gp.memset(causal[:], 0.0))
            link(gp.affine_select(out=causal[:], in_=causal[:], compare_op=ALU.is_ge, fill=NEG1, base=0,
                                  pattern=[[-1, P]], channel_multiplier=1))
            link(gp.memset(avg, 1.0 / P))
            link(gp.memset(hmask[:], 0.25))
            link(gp.affine_select(out=hmask[:], in_=hmask[:], compare_op=ALU.is_ge, fill=0.0, base=0,
                                  pattern=[[-HD, H]], channel_multiplier=1))
            link(gp.affine_select(out=hmask[:], in_=hmask[:], compare_op=ALU.is_ge, fill=0.0, base=HD - 1,
                                  pattern=[[HD, H]], channel_multiplier=-1))
            for h in range(H):
                link(gp.memset(hoff[:, h:h + 1], float(h * NKV)))
            for i in range(NC):
                link(gp.memset(iota[:, i:i + 1], float(i)))
            assert done[0] == NCONST
            gp.wait_ge(prep_pe, 1)

            def gather(m, s, signal):
                gp.wait_ge(row_ready, m + (1 + 2 * SLOTS))
                gp.wait_ge(sum_ready, m + (1 + 2 * SLOTS))
                gp.sem_inc(turn[1], 1)
                for j in range(TOPK):
                    gp.indirect_dma_start(out=G[s][:, j, :], out_offset=None, in_=a["table"][:, :],
                                          in_offset=bass.IndirectOffsetOnAxis(ap=row[s][:, j:j + 1], axis=0)
                                          ).then_inc(signal, 16)

            with gp.Fori(0, NB * SLOTS - 2, 2) as m:
                for s in range(2):
                    gather(m + s, s, gathered[s])
            for s in range(2):
                gather(NB * SLOTS - 2 + s, s, gathered_last[s])

        @block.tensor
        def _(pe):
            pe.wait_ge(ld_w, 16 * len(LOADS))
            pe.wait_ge(const_ready, NCONST)
            for i in range(2 * H):
                last = pe.matmul(bank[i // 4][:, (i % 4) * P:(i % 4 + 1) * P], pkq[:, i * P:(i + 1) * P],
                                 pkk[:, i * P:(i + 1) * P], start=True, stop=True)
            last.then_inc(prep_pe, 1)
            pe.wait_ge(prep_dve, 1)
            pe.matmul(bank[6][:, 0:P], avg, wf[:], start=True, stop=True)
            pe.matmul(bank[6][:, P:2 * P], hT[:, 0:P], wft, start=True, stop=True).then_inc(prep_pe, 1)
            pe.wait_ge(prep_act, 4)
            pe.wait_ge(prep_dve, 2)

            def transposes(dst, src, ready, n=TILES):
                for t in range(n):
                    last = pe.transpose(dst[:, t * P:(t + 1) * P], src[:, t * P:(t + 1) * P], ident[:])
                last.then_inc(ready, 1)

            def out_projection(g, w, oT_ps, oT_sb, proj, p):
                transposes(bank[0], oo[g][:].rearrange("p t c -> p (t c)"), oT_ps)
                pe.wait_ge(oT_sb, p)
                for t in range(TILES):
                    last = pe.matmul(bank[1][:, t * P:(t + 1) * P], oT[:, t * P:(t + 1) * P], w[:], start=True, stop=True)
                last.then_inc(proj, 1)

            def qkv(wq, wk, wv, src, ready):
                pe.matmul(bank[5][:], wq[:], src[:], start=True, stop=True)
                pe.matmul(bank[6][:], wk[:], src[:], start=True, stop=True)
                for t in range(TILES):
                    last = pe.matmul(bank[7][:, t * P:(t + 1) * P], src[:, t * P:(t + 1) * P], wv[:], start=True, stop=True)
                last.then_inc(ready, 1)

            def boundary(p, like):
                if like > 1:
                    pe.wait_ge(act_done, p - 1)
                    pe.wait_ge(dve_done, p - 1)
                if active("F", like - 1):
                    for q in (h2t_ready, y_ready):
                        pe.sem_inc(q, SLOTS - ITERS)
                if active("B", like - 1):
                    out_projection(1, w1o, g1_oT, g1_oTsb, g1_pr, p)
                if active("C", like - 1):
                    pe.wait_ge(c_xn, p)
                    transposes(bank[2], xn[:].rearrange("p t c -> p (t c)"), c_xT)
                    pe.wait_ge(c_xTsb, p)
                    qkv(w1q, w1k, w1v, oT, c_q)
                    pe.wait_ge(c_qsb, p)
                if active("A", like - 1):
                    out_projection(0, w0o, g0_oT, g0_oTsb, g0_pr, p)
                    pe.wait_ge(g0_xn, p)
                    transposes(bank[2], xn[:].rearrange("p t c -> p (t c)"), g0_xT)
                    pe.wait_ge(g0_xTsb, p)
                if active("A", like):
                    pe.wait_ge(i_xn, p)
                    transposes(bank[2], xn[:].rearrange("p t c -> p (t c)"), i_xT)
                    pe.wait_ge(i_xTsb, p)
                    qkv(w0q, w0k, w0v, oT, i_q)
                    pe.wait_ge(i_qsb, p)
                    pe.wait_ge(i_v, p)
                if active("T", like):
                    pe.wait_ge(g0_xTsb, p)
                if active("C", like):
                    pe.wait_ge(t_cp, p)

            def slot(tile, s, h, n, st, p, like, cbase):
                v1 = snap(pe, n + 1)
                nk = (tile + 1) * P
                cur = slice(tile * P, (tile + 1) * P)

                def scores(g):
                    pe.wait_ge(qz_ready[g], v1)
                    pe.matmul(SC[g][:], qz[g][:], kT[g][:], start=True, stop=False)
                    pe.matmul(SC[g][:], identh[:], maskt[g][tile % 2][:], start=False, stop=True).then_inc(sc_ready[g], 1)

                def probs_T(g, cnt):
                    pe.wait_ge(pr_ready[g], v1)
                    transposes(SC[g], pr[g], pt_ready[g], cnt)

                def head_av(g):
                    pe.wait_ge(ptsb_ready[g], v1)
                    for kt in range(TILES):
                        last = pe.matmul(psO[g], prT[g][:, kt * P:(kt + 1) * P], vv[g][:, kt, bass.ds(h * HD, HD)],
                                         start=kt == 0, stop=kt == TILES - 1)
                    last.then_inc(av_ready[g], 1)

                def sums(half):
                    if half == 0 and "T" in st:
                        pe.wait_ge(gathered[s], (n - s) * P - (2 * SLOTS + 2) * P + 256)
                    elif half == 0:
                        pe.wait_ge(gathered_last[s], 16 * TOPK)
                    pe.wait_ge(dg_ready[half], v1)
                    for j in range(half * 8, half * 8 + 8):
                        pe.matmul(psK[s], G[s][:, j, 0:D], dg[s][:, j, :], start=j == 0, stop=j == TOPK - 1,
                                  skip_group_check=True)
                        last = pe.matmul(psV[s], dg[s][:, j, :], G[s][:, j, D:2 * D], start=False, stop=j == TOPK - 1,
                                         skip_group_check=True)
                    if half:
                        last.then_inc(sum_ready, 1)

                if s == 0:
                    for g in range(2):
                        if GS[g] in st:
                            pe.wait_ge(mask_ready[g], (p - 1 - LAG[GS[g]]) * TILES + tile + 1)
                if "A" in st:
                    scores(0)
                if "B" in st:
                    scores(1)
                if "C" in st:
                    pe.wait_ge(wqs_ready, v1)
                    pe.matmul(psq, wqs[:], xcT[:, cur], start=True, stop=True).then_inc(q_ready, 1)
                if "T" in st:
                    pe.matmul(psS, xtT[:, cur], simw[:, bass.ds(h, 1), :, :].rearrange("p a b c -> p (a b c)"),
                              start=True, stop=True).then_inc(sim_ready, 1)
                if "C" in st:
                    pe.wait_ge(qs_ready, v1)
                    kv = KT[:].rearrange("p (u c) -> p u c", c=P)
                    src = kv[:, bass.ds(cbase + h, tile * H + 1), :][:, 0:tile * H + 1:H, :] if tile else \
                        kv[:, bass.ds(cbase + h, 1), :]
                    pe.matmul(SC[2][:, 0:nk], qs[:], src, start=True, stop=False)
                    pe.matmul(SC[2][:, cur], identh[:], causal[:], start=False, stop=True).then_inc(sc_ready[2], 1)
                if "W" in st:
                    pe.wait_ge(sumsb_ready, n - 1)
                    sums(0)
                if "A" in st:
                    probs_T(0, TILES)
                if "B" in st:
                    probs_T(1, TILES)
                if "F" in st:
                    pe.wait_ge(h2_ready, v1)
                    transposes(psH, h1[:].rearrange("p t c -> p (t c)"), h2t_ready)
                if "A" in st:
                    head_av(0)
                if "B" in st:
                    head_av(1)
                if "C" in st:
                    probs_T(2, tile + 1)
                if "F" in st:
                    pe.wait_ge(h2tsb_ready, v1)
                    for t in range(TILES):
                        last = pe.matmul(psY[:, t * P:(t + 1) * P], hT[:, t * P:(t + 1) * P], wf[:], start=True, stop=True)
                    last.then_inc(y_ready, 1)
                if "C" in st:
                    pe.wait_ge(ptsb_ready[2], v1)
                    for kt in range(tile + 1):
                        last = pe.matmul(psC, prT[2][:, kt * P:(kt + 1) * P], VV[:, bass.ds((cbase + kt * H + h) * P, P)],
                                         start=kt == 0, stop=kt == tile)
                    last.then_inc(av_ready[2], 1)
                if "W" in st:
                    sums(1)
                if "C" in st:
                    pe.wait_ge(oc_ready, v1)
                    transposes(psCT, oc, oct_ready, 1)
                    pe.wait_ge(octsb_ready, v1)
                    if "F" in st:
                        pe.wait_ge(f_ready, v1)
                    pe.matmul(psw, ocT[:], wco[:, bass.ds(h, 1), :].rearrange("p a b -> p (a b)"),
                              start=True, stop=True).then_inc(wo_ready, 1)

            def one(p, like):
                boundary(p, like)
                cbase = snap(pe, ((p + 1) % 2) * SLOTS)
                slots(pe, p, like, lambda *v: slot(*v, p, like, cbase))
                pe.drain().then_inc(pe_done, 1)
            periods(pe, one)
            pe.wait_ge(act_done, LAST)
            pe.wait_ge(dve_done, LAST)

        @block.scalar
        def _(act):
            act.wait_ge(prep_pe, 1)
            sw = simw[:].rearrange("p h a k -> p a h k")
            for i in range(4):
                act.activation(sw[:, i // 2, 4 * (i % 2):4 * (i % 2) + 4, :],
                               bank[i][:].rearrange("p (h k) -> p h k", k=P), ACT.Copy).then_inc(prep_act, 1)

            def boundary(p, like):
                if like > 1:
                    act.wait_ge(pe_done, p - 1)
                    act.wait_ge(dve_done, p - 1)
                else:
                    act.wait_ge(prep_dve, 2)
                if active("F", like - 1):
                    for q in (th_ready, sg_ready, h2tsb_ready):
                        act.sem_inc(q, SLOTS - ITERS)
                if active("B", like - 1):
                    act.wait_ge(g1_oT, p)
                    act.activation(oT[:], bank[0][:], ACT.Copy).then_inc(g1_oTsb, 1)
                if active("C", like - 1):
                    act.wait_ge(c_xT, p)
                    act.activation(oT[:], bank[2][:], ACT.Copy).then_inc(c_xTsb, 1)
                    act.wait_ge(c_q, p)
                    act.activation(qT[1][:], bank[5][:], ACT.Copy)
                    act.activation(kT[1][:], bank[6][:], ACT.Copy)
                    act.activation(vv[1][:].rearrange("p t c -> p (t c)"), bank[7][:], ACT.Copy).then_inc(c_qsb, 1)
                if active("C", like):
                    act.activation(xcT[:], xtT[:], ACT.Copy).then_inc(t_cp, 1)
                if active("A", like - 1):
                    act.wait_ge(g0_oT, p)
                    act.activation(oT[:], bank[0][:], ACT.Copy).then_inc(g0_oTsb, 1)
                    act.wait_ge(g0_xT, p)
                    act.activation(xtT[:], bank[2][:], ACT.Copy).then_inc(g0_xTsb, 1)
                if active("A", like):
                    act.wait_ge(i_xT, p)
                    act.activation(oT[:], bank[2][:], ACT.Copy).then_inc(i_xTsb, 1)
                    act.wait_ge(i_q, p)
                    act.activation(qT[0][:], bank[5][:], ACT.Identity, bias=b0q[:])
                    act.activation(kT[0][:], bank[6][:], ACT.Identity, bias=b0k[:]).then_inc(i_qsb, 1)

            def slot(tile, s, h, n, st, p, like):
                v1 = snap(act, n + 1)
                nk = (tile + 1) * P
                cur = slice(tile * P, (tile + 1) * P)

                def head_q(g):
                    act.activation(qz[g][:], qT[g][:, cur], ACT.Copy, scale=hmask[:, bass.ds(h, 1)]).then_inc(qz_ready[g], 1)

                def probs(g, cols):
                    act.wait_ge(nm_ready[g], v1)
                    src = pr[1][:] if g == 1 else SC[g][:, 0:cols]
                    act.activation(pr[g][:, 0:cols], src, ACT.Exp, bias=nm[g][:], accum_out=rs[g][:]).then_inc(pr_ready[g], 1)

                def copy_T(g, cols):
                    act.wait_ge(pt_ready[g], v1)
                    act.activation(prT[g][:, 0:cols], SC[g][:, 0:cols], ACT.Copy).then_inc(ptsb_ready[g], 1)

                def diags(half):
                    for j in range(half * 8, half * 8 + 8):
                        last = act.activation(dg[s][:, j, :], ident[:], ACT.Copy, scale=wt[s][:, j:j + 1])
                    last.then_inc(dg_ready[half], 1)

                if "A" in st:
                    head_q(0)
                if "B" in st:
                    head_q(1)
                if "C" in st:
                    act.activation(wqs[:], wcq[:, bass.ds(h * D, D)], ACT.Copy).then_inc(wqs_ready, 1)
                if "F" in st:
                    act.wait_ge(f_ready, n)
                    act.activation(sg[:], hh[:], ACT.Tanh).then_inc(th_ready, 1)
                if "W" in st:
                    act.wait_ge(wt_ready, n - 1)
                    act.wait_ge(sum_ready, n - 1)
                    diags(0)
                if "C" in st:
                    act.wait_ge(q_ready, v1)
                    act.activation(qs[:], psq, ACT.Copy, scale=float(D) ** -0.5).then_inc(qs_ready, 1)
                if "A" in st:
                    probs(0, S)
                if "B" in st:
                    probs(1, S)
                if "F" in st:
                    act.wait_ge(h1_ready, v1)
                    act.activation(sg[:], h1[:], ACT.Tanh, scale=0.5).then_inc(sg_ready, 1)
                if "A" in st:
                    copy_T(0, S)
                if "B" in st:
                    copy_T(1, S)
                if "C" in st:
                    probs(2, nk)
                if "W" in st:
                    diags(1)
                if "F" in st:
                    act.wait_ge(h2t_ready, v1)
                    act.activation(hT[:], psH[:], ACT.Copy).then_inc(h2tsb_ready, 1)
                if "C" in st:
                    copy_T(2, nk)
                if "T" in st:
                    act.wait_ge(ng_ready, v1)
                    act.activation(ew[:], fin[:], ACT.Exp, bias=negm[:], accum_out=tsum[:]).then_inc(ew_ready, 1)
                if "C" in st:
                    act.wait_ge(av_ready[2], v1)
                    act.wait_ge(rc_ready, v1)
                    act.activation(oc[:], psC, ACT.Copy, scale=rr[2][:]).then_inc(oc_ready, 1)
                if "W" in st:
                    act.wait_ge(sum_ready, v1)
                    u = snap(act, ((n - 2) % (2 * SLOTS)) * P)
                    act.activation(KT[:, bass.ds(u, P)], psK[s], ACT.Copy)
                    act.activation(VV[:, bass.ds(u, P)], psV[s], ACT.Copy).then_inc(sumsb_ready, 1)
                if "C" in st:
                    act.wait_ge(oct_ready, v1)
                    act.activation(ocT[:], psCT, ACT.Copy).then_inc(octsb_ready, 1)

            def one(p, like):
                boundary(p, like)
                if active("A", like):
                    act.wait_ge(i_qsb, p)
                if active("B", like):
                    act.wait_ge(c_qsb, p)
                slots(act, p, like, lambda *v: slot(*v, p, like))
                act.drain().then_inc(act_done, 1)
            periods(act, one)

        @block.vector
        def _(dve):
            chain = [0]

            def put(ins):
                ins.then_inc(dchain, 1)
                chain[0] += 1
                return chain[0]

            def need(v):
                dve.wait_ge(dchain, v)

            def restart():
                if chain[0]:
                    dve.wait_ge(dchain, chain[0])
                dve.sem_clear(dchain)
                chain[0] = 0

            def rsqrt_steps(src, eps):
                yield lambda: dve.tensor_scalar(va[:], src, eps, None, ALU.add)
                yield lambda: dve.tensor_scalar(yb[:].bitcast(i32), va[:].bitcast(i32), 1, None, ALU.logical_shift_right)
                yield lambda: dve.tensor_scalar(ya[:].bitcast(i32), yb[:].bitcast(i32), -1.0, float(0x5f3759df), ALU.mult, ALU.add)
                for _ in range(3):
                    yield lambda: dve.tensor_tensor(yb[:], ya[:], ya[:], ALU.mult)
                    yield lambda: dve.scalar_tensor_tensor(out=yc[:], in0=yb[:], scalar=-0.5, in1=va[:], op0=ALU.mult, op1=ALU.mult)
                    yield lambda: dve.scalar_tensor_tensor(out=ya[:], in0=yc[:], scalar=1.5, in1=ya[:], op0=ALU.add, op1=ALU.mult)

            def rsqrt(src, eps):
                for step in rsqrt_steps(src, eps):
                    need(put(step()))

            def layernorm(dst, src, ready):
                for t in range(TILES):
                    a = put(dve.bn_stats(stats[:, t, :], src[:, t, :]))
                need(a)
                for t in range(TILES):
                    a = put(dve.bn_aggr(mv[:, t, :], stats[:, t, :]))
                need(a)
                rsqrt(mv[:, :, 1], EPS)
                for t in range(TILES):
                    last = dve.tensor_scalar(dst[:, t, :], src[:, t, :], mv[:, t, 0:1], ya[:, t:t + 1], ALU.subtract, ALU.mult)
                last.then_inc(ready, 1)

            dve.wait_ge(ld_w, 16 * len(LOADS))
            dve.wait_ge(const_ready, NCONST)
            need(put(dve.memset(hT[:, P:2 * P], 1.0)))
            dve.tensor_scalar(hT[:, 0:P], hT[:, P:2 * P], lnb[:], None, ALU.mult)
            dve.tensor_scalar(wf[:], wft, lnw[:], None, ALU.mult).then_inc(prep_dve, 1)
            dve.wait_ge(prep_pe, 2)
            dve.tensor_tensor(wf[:], wf[:], bank[6][:, 0:P], ALU.subtract)
            dve.tensor_tensor(bf[:], bf[:], bank[6][:, P:2 * P], ALU.add).then_inc(prep_dve, 1)

            def boundary(p, like):
                restart()
                if like > 1:
                    dve.wait_ge(pe_done, p - 1)
                    dve.wait_ge(act_done, p - 1)
                if active("F", like - 1):
                    for q in (h1_ready, h2_ready):
                        dve.sem_inc(q, SLOTS - ITERS)
                    dve.tensor_tensor(xf[:], xf[:], hh[:], ALU.add).then_inc(o_ready, 1)
                if active("B", like - 1):
                    dve.wait_ge(g1_pr, p)
                    if active("F", like - 1):
                        dve.wait_ge(stored, (p - 5) * 16)
                    need(put(dve.tensor_tensor(xf[:].rearrange("p t c -> p (t c)"), bank[1][:],
                                               xg[:].rearrange("p t c -> p (t c)"), ALU.add)))
                    dve.sem_inc(f_ready, 1)
                    layernorm(hh, xf, f_ready)
                if active("C", like - 1):
                    need(put(dve.tensor_copy(xg[:], xc[:])))
                    layernorm(xn, xg, c_xn)
                if active("C", like):
                    need(put(dve.tensor_copy(xc[:], xa[:])))
                if active("A", like - 1):
                    dve.wait_ge(g0_pr, p)
                    if active("C", like - 1):
                        dve.wait_ge(c_xT, p)
                    need(put(dve.tensor_tensor(xa[:].rearrange("p t c -> p (t c)"), bank[1][:],
                                               x0[:].rearrange("p t c -> p (t c)"), ALU.add)))
                    need(put(dve.tensor_tensor(xa[:], xa[:], b0o[:].rearrange("p (a c) -> p a c", a=1).to_broadcast([P, TILES, D]), ALU.add)))
                    layernorm(xn, xa, g0_xn)
                if active("A", like):
                    if active("A", like - 1):
                        dve.wait_ge(g0_xT, p)
                    dve.wait_ge(ld_x, p * 16)
                    dve.tensor_copy(x0[:], xin[:]).then_inc(x_used, 1)
                    layernorm(xn, xin, i_xn)
                    dve.wait_ge(i_q, p)
                    dve.tensor_tensor(vv[0][:], bank[7][:].rearrange("p (t c) -> p t c", t=TILES),
                                      b0v[:].rearrange("p (a c) -> p a c", a=1).to_broadcast([P, TILES, D]),
                                      ALU.add).then_inc(i_v, 1)

            def masks(p, like, t):
                for g in range(2):
                    if active(GS[g], like):
                        first = 1 + LAG[GS[g]]
                        dve.wait_ge(ld_adj[g][t % 2], (p - first) * 32 + (t // 2 + 1) * 16)
                        dve.tensor_scalar(maskt[g][t % 2][:], adjt[g][t % 2][:], 0.0, (NEG0, NEG1)[g],
                                          (ALU.is_le, ALU.is_equal)[g], ALU.mult).then_inc(mask_ready[g], 1)

            def slot(tile, s, h, n, st, p, like):
                v1 = snap(dve, n + 1)
                nk = (tile + 1) * P
                restart()

                def negmax(g, src):
                    dve.tensor_reduce(nm[g][:], src, AX, ALU.max, negate=True).then_inc(nm_ready[g], 1)

                if "F" in st:
                    dve.wait_ge(th_ready, v1)
                    dve.scalar_tensor_tensor(out=h1[:], in0=sg[:], scalar=0.01, in1=hh[:], op0=ALU.mult,
                                             op1=ALU.add).then_inc(h1_ready, 1)
                if "A" in st:
                    dve.wait_ge(sc_ready[0], v1)
                    negmax(0, SC[0][:])
                if "B" in st:
                    dve.wait_ge(sc_ready[1], v1)
                    c = put(dve.scalar_tensor_tensor(out=pr[1][:], in0=adjt[1][tile % 2][:], scalar=we[:, bass.ds(h, 1)],
                                                     in1=SC[1][:], op0=ALU.mult, op1=ALU.add))
                if "T" in st:
                    dve.wait_ge(sim_ready, v1)
                    dve.sem_inc(turn[0], 1)
                    a0 = put(dve.max(top[:, 0, 0:8], psS[:, 0:128]))
                    a1 = put(dve.max(top[:, 1, 0:8], psS[:, 128:256]))
                if "B" in st:
                    need(c)
                    negmax(1, pr[1][:])
                if "T" in st:
                    need(a1)
                    a0 = put(dve.match_replace(rest[:, 0, :], top[:, 0, 0:8], psS[:, 0:128], LOW))
                    a1 = put(dve.match_replace(rest[:, 1, :], top[:, 1, 0:8], psS[:, 128:256], LOW))
                    dve.max_index(topi[:, 0, 0:8], top[:, 0, 0:8], psS[:, 0:128])
                    dve.max_index(topi[:, 1, 0:8], top[:, 1, 0:8], psS[:, 128:256])
                    need(a1)
                    a0 = put(dve.max(top[:, 0, 8:16], rest[:, 0, :]))
                    a1 = put(dve.max(top[:, 1, 8:16], rest[:, 1, :]))
                if "C" in st:
                    dve.wait_ge(sc_ready[2], v1)
                    negmax(2, SC[2][:, 0:nk])
                if "T" in st:
                    need(a1)
                    dve.max_index(topi[:, 0, 8:16], top[:, 0, 8:16], rest[:, 0, :])
                    ai = put(dve.max_index(topi[:, 1, 8:16], top[:, 1, 8:16], rest[:, 1, :]))
                if "F" in st:
                    dve.wait_ge(sg_ready, v1)
                    dve.scalar_tensor_tensor(out=h1[:], in0=sg[:], scalar=1.0, in1=h1[:], op0=ALU.add,
                                             op1=ALU.mult).then_inc(h2_ready, 1)
                if "T" in st:
                    need(ai)
                    at = 0
                    for i0, r, c in GROUPS:
                        def grid(t, k):
                            v = t[:, 0, i0:i0 + r].rearrange("p (r c) -> p r c", c=1).to_broadcast([P, r, c]) if k == 0 else \
                                t[:, 1, 0:c].rearrange("p (r c) -> p r c", r=1).to_broadcast([P, r, c])
                            return v
                        dst = slice(at, at + r * c)
                        dve.tensor_tensor(cand[:, dst].rearrange("p (r c) -> p r c", c=c), grid(top, 0), grid(top, 1), ALU.add)
                        ac = put(dve.scalar_tensor_tensor(out=candi[:, dst].rearrange("p (r c) -> p r c", c=c), in0=grid(topi, 1),
                                                          scalar=float(NKEYS), in1=grid(topi, 0), op0=ALU.mult, op1=ALU.add))
                        at += r * c
                if "F" in st:
                    dve.wait_ge(h2_ready, v1)
                    for t in range(TILES):
                        a = put(dve.bn_stats(stats[:, t, :], h1[:, t, :]))
                newton = []
                if "F" in st:
                    need(a)
                    for t in range(TILES):
                        a = put(dve.bn_aggr(mv[:, t, :], stats[:, t, :]))
                    newton = list(rsqrt_steps(mv[:, :, 1], 4 * EPS))
                    nw = [a]

                def newton_step(k=1):
                    for _ in range(k):
                        if newton:
                            need(nw[0])
                            nw[0] = put(newton.pop(0)())

                newton_step()
                if "T" in st:
                    need(ac)
                    b = put(dve.max(fin[:, 0:8], cand[:]))
                    newton_step()
                    need(b)
                    dve.max_index(pos[:, 0:8], fin[:, 0:8], cand[:])
                    b = put(dve.match_replace(candr[:], fin[:, 0:8], cand[:], LOW))
                    newton_step()
                    need(b)
                    b = put(dve.max(fin[:, 8:16], candr[:]))
                    newton_step()
                    need(b)
                    dve.tensor_scalar(negm[:], fin[:, 0:1], -1.0, None, ALU.mult).then_inc(ng_ready, 1)
                    b = put(dve.max_index(pos[:, 8:16], fin[:, 8:16], candr[:]))
                newton_step(20)
                for g in range(3):
                    if "ABC"[g] in st:
                        dve.wait_ge(pr_ready[g], v1)
                        r = dve.reciprocal(rr[g][:], rs[g][:])
                        if g == 2:
                            r.then_inc(rc_ready, 1)
                        else:
                            lr = put(r)
                if "T" in st:
                    need(b)
                    b = put(dve.tensor_tensor(hit[:], pos[:].rearrange("p (j c) -> p j c", c=1).to_broadcast([P, TOPK, NC]),
                                              iota[:].rearrange("p (j c) -> p j c", j=1).to_broadcast([P, TOPK, NC]), ALU.is_equal))
                for g in range(2):
                    if GS[g] in st:
                        dve.wait_ge(av_ready[1 if "B" in st else 0], v1)
                        need(lr)
                        dve.tensor_scalar(oo[g][:, tile, bass.ds(h * HD, HD)], psO[g], rr[g][:], None, ALU.mult)
                if "T" in st:
                    need(b)
                    b = put(dve.tensor_tensor(hit[:], hit[:], candi[:].rearrange("p (j c) -> p j c", j=1)
                                              .to_broadcast([P, TOPK, NC]), ALU.mult))
                if "F" in st:
                    dve.wait_ge(y_ready, v1)
                    need(nw[0])
                    for t in range(TILES):
                        last = dve.scalar_tensor_tensor(out=hh[:, t, :], in0=psY[:, t * P:(t + 1) * P], scalar=ya[:, t:t + 1],
                                                        in1=bf[:], op0=ALU.mult, op1=ALU.add)
                    last.then_inc(f_ready, 1)
                if "T" in st:
                    need(b)
                    b = put(dve.tensor_reduce(rowf[:], hit[:], AX, ALU.add))
                    dve.wait_ge(ew_ready, v1)
                    b2 = put(dve.reciprocal(trec[:], tsum[:]))
                    if not (like == 2 and tile == 0 and isinstance(h, int) and h < 2):
                        dve.wait_ge(gathered[s], (n - s) * P - (2 * SLOTS + 2) * P + 256)
                        dve.wait_ge(dg_ready[1], v1)
                    need(b)
                    dve.tensor_scalar(row[s][:], rowf[:], hoff[:, bass.ds(h, 1)], None, ALU.add).then_inc(row_ready, 1)
                    need(b2)
                    dve.tensor_scalar(wt[s][:], ew[:], trec[:], None, ALU.mult).then_inc(wt_ready, 1)
                if "C" in st:
                    dve.wait_ge(wo_ready, v1)
                    put(dve.tensor_tensor(xc[:, tile, :], psw, xc[:, tile, :], ALU.add))

            def one(p, like):
                boundary(p, like)
                at = [-1]

                def tile_slot(tile, *v):
                    if tile != at[0]:
                        at[0] = tile
                        masks(p, like, tile)
                    slot(tile, *v, p, like)

                slots(dve, p, like, tile_slot)
                dve.drain().then_inc(dve_done, 1)

            periods(dve, one)
            dve.wait_ge(act_done, LAST)
            dve.tensor_tensor(xf[:], xf[:], hh[:], ALU.add).then_inc(o_ready, 1)


def kernel(**i):
    import concourse.bacc as bacc
    from concourse.bass_utils import run_bass_kernel_spmd

    i = {k: np.asarray(v) for k, v in i.items()}
    arrays = dict(
        x=i["x"], adj=i["adj"],
        w0q=i["L0_gnn_Wq"], w0k=i["L0_gnn_Wk"], w0v=i["L0_gnn_Wv"], w0o=i["L0_gnn_Wo"],
        b0q=i["L0_gnn_bq"], b0k=i["L0_gnn_bk"], b0v=i["L0_gnn_bv"], b0o=i["L0_gnn_bo"],
        pkq=i["L0_ffn_Wq_pk"].reshape(D, 2 * H, DK).transpose(2, 1, 0).reshape(DK, 2 * H * D),
        pkk=i["L0_ffn_pk_keys"].transpose(3, 0, 2, 1).reshape(DK, 2 * H * NKEYS),
        wcq=i["L0_ffn_Wq"], wco=i["L0_ffn_Wo"],
        table=np.concatenate([i["L0_ffn_keys_table"], i["L0_ffn_values_table"]], axis=1),
        w1q=i["L1_gnn_W_q"].T, w1k=i["L1_gnn_W_k"].T, w1v=i["L1_gnn_W_v"].T, w1o=i["L1_gnn_W_o"].T,
        we=i["L1_gnn_W_e"].reshape(H), lnw=i["L1_ffn_ln_w"], lnb=i["L1_ffn_ln_b"],
        wft=i["L1_ffn_W"].T, bf=i["L1_ffn_b"])
    nc = bacc.Bacc("TRN2", target_bir_lowering=False, num_devices=1)
    feeds, args = {}, {}
    for name, v in arrays.items():
        v = np.ascontiguousarray(v)
        feeds[f"in_{name}"] = v
        args[name] = nc.dram_tensor(f"in_{name}", v.shape, mybir.dt.from_np(v.dtype), kind="ExternalInput").ap()
    out = nc.dram_tensor("out_y", (NB, S, D), mybir.dt.float32, kind="ExternalOutput").ap()
    build(nc, args, out)
    r = run_bass_kernel_spmd(nc, [feeds], core_ids=[0])
    return r.results[0]["out_y"]
```

```python
import numpy as np
import concourse.bass as bass
from concourse import mybir
from contextlib import ExitStack

P = 128
NB, S, D = 16, 512, 128
TILES = S // P
H, HD = 8, 16
NKEYS, DK, TOPK = 128, 64, 16
NKV = NKEYS * NKEYS
ITERS = 30
SLOTS = TILES * H
GROUPS = ((0, 1, 16), (1, 1, 8), (2, 2, 5), (4, 4, 3), (8, 8, 1))
NC = sum(r * c for _, r, c in GROUPS)
LAG = {"A": 0, "T": 1, "C": 2, "B": 3, "F": 4}
NEG0 = -9.0e15
NEG1 = -1.0e37
LOW = -3.0e38
EPS = 1e-5
NCONST = 9 + H + NC


def active(stage, period):
    return 0 <= period - 1 - LAG[stage] < NB


def build(nc, a, out):
    f32, bf16, u32, i32 = mybir.dt.float32, mybir.dt.bfloat16, mybir.dt.uint32, mybir.dt.int32
    ALU = mybir.AluOpType
    ACT = mybir.ActivationFunctionType
    AX = mybir.AxisListType.X
    LAST = NB + 4

    ctx = ExitStack()
    with ctx:
        x, adj = a["x"], a["adj"]

        def sb(name, shape, dt=f32):
            return ctx.enter_context(nc.sbuf_tensor(name, shape, dt))

        def pb(name, shape, dt=f32):
            return ctx.enter_context(nc.psum_tensor(name, shape, dt))

        def sem(name):
            return ctx.enter_context(nc.semaphore(name))

        starts = []

        def slot_sem(name, stage):
            s = sem(name)
            starts.append((s, SLOTS * (1 + LAG[stage])))
            return s

        def period_sem(name, first):
            s = sem(name)
            if first > 1:
                starts.append((s, first - 1))
            return s

        ident = sb("ident", [P, P])
        identh = sb("identh", [P, P], bf16)
        causal = sb("causal", [P, P], bf16)
        hmask = sb("hmask", [P, H])
        hoff = sb("hoff", [P, H])
        iota = sb("iota", [P, NC])
        we = sb("we", [P, H])
        w0q, w0k, w0v, w0o = (sb(n, [P, P]) for n in ("w0q", "w0k", "w0v", "w0o"))
        w1q, w1k, w1v, w1o = (sb(n, [P, P]) for n in ("w1q", "w1k", "w1v", "w1o"))
        b0q, b0k = sb("b0q", [P, 1]), sb("b0k", [P, 1])
        b0v, b0o = sb("b0v", [P, P]), sb("b0o", [P, P])
        simw = sb("simw", [P, H, 2, NKEYS])
        wcq = sb("wcq", [P, H * D])
        wco = sb("wco", [P, H, D])
        wf, bf = sb("wf", [P, P]), sb("bf", [P, P])
        lnw, lnb = sb("lnw", [P, 1]), sb("lnb", [P, 1])

        xin, x0, xa = sb("xin", [P, TILES, D]), sb("x0", [P, TILES, D]), sb("xa", [P, TILES, D])
        xg, xf = sb("xg", [P, TILES, D]), sb("xf", [P, TILES, D])
        xc = sb("xc", [P, TILES, D])
        qT = [sb(f"qT{g}", [P, S]) for g in range(2)]
        kT = [sb(f"kT{g}", [P, S]) for g in range(2)]
        vv = [sb(f"vv{g}", [P, TILES, D]) for g in range(2)]
        oo = [sb(f"oo{g}", [P, TILES, D]) for g in range(2)]
        adjt = [[sb(f"adj{g}{i}", [P, S]) for i in range(2)] for g in range(2)]
        maskt = [[sb(f"mask{g}{i}", [P, S], bf16) for i in range(2)] for g in range(2)]
        qz = [sb(f"qz{g}", [P, P]) for g in range(2)]
        pr = [sb(f"pr{g}", [P, S]) for g in range(3)]
        prT = [sb(f"prT{g}", [P, S]) for g in range(3)]
        nm = [sb(f"nm{g}", [P, 1]) for g in range(3)]
        rs = [sb(f"rs{g}", [P, 1]) for g in range(3)]
        rr = [sb(f"rr{g}", [P, 1]) for g in range(3)]

        xtT, xcT = sb("xtT", [P, S]), sb("xcT", [P, S])
        top = sb("top", [P, 2, TOPK])
        topi = sb("topi", [P, 2, TOPK], u32)
        cand, candr, candi = sb("cand", [P, NC]), sb("candr", [P, NC]), sb("candi", [P, NC])
        fin = sb("fin", [P, TOPK])
        pos = sb("pos", [P, TOPK], u32)
        hit = sb("hit", [P, TOPK, NC])
        rest = hit[:].rearrange("p j c -> p (j c)")[:, 0:2 * NKEYS].rearrange("p (a k) -> p a k", a=2)
        rowf = sb("rowf", [P, TOPK])
        negm, tsum, trec = sb("negm", [P, 1]), sb("tsum", [P, 1]), sb("trec", [P, 1])
        ew = sb("ew", [P, TOPK])
        row = [sb(f"row{i}", [P, TOPK], u32) for i in range(2)]
        wt = [sb(f"wt{i}", [P, TOPK]) for i in range(2)]
        G = [sb(f"G{i}", [P, TOPK, 2 * D]) for i in range(2)]
        dg = [sb(f"dg{i}", [P, TOPK, P]) for i in range(2)]
        KT = sb("KT", [P, 2 * SLOTS * P])
        VV = sb("VV", [P, 2 * SLOTS * P])

        wqs, qs, ocT = sb("wqs", [P, P]), sb("qs", [P, P]), sb("ocT", [P, P])
        oc = qs

        hh, h1, sg = sb("hh", [P, TILES, D]), sb("h1", [P, TILES, D]), sb("sg", [P, TILES, D])
        hT = sb("hT", [P, S])
        avg, wft = hh[:, 0, :], sg[:, 0, :]
        stats, mv = sb("stats", [P, 2 * TILES, 6]), sb("mv", [P, 2 * TILES, 2])
        va, ya, yb, yc = (sb(n, [P, 2 * TILES]) for n in ("va", "ya", "yb", "yc"))
        tokens = lambda t: t[:].rearrange("p (t c) -> p t c", t=TILES)
        xnC, xnI, xnA = pr
        oTB, oTA, xTC = prT
        xTI = hT

        bank = [pb(f"bank{i}", [P, 512]) for i in range(8)]
        SC = bank[0:3]
        psq = psC = psCT = SC[2][:, 0:128]
        psK = [b[:, 0:128] for b in (bank[3], bank[6])]
        psV = [b[:, 128:256] for b in (bank[3], bank[6])]
        psS = bank[4][:, 0:256]
        psO = [bank[7][:, 0:HD], bank[7][:, HD:2 * HD]]
        psH = psY = bank[5]
        psw = bank[5][:, 0:128]

        GS = ("A", "B")
        ld_w = sem("weights_loaded")
        ld_x = sem("x_loaded")
        ld_adj = [[sem(f"adj{g}{i}_loaded") for i in range(2)] for g in GS]
        mask_ready = [sem(f"mask{g}_ready") for g in GS]
        stored = sem("out_stored")
        const_ready = sem("const_ready")
        prep_pe, prep_act, prep_dve = sem("prep_pe"), sem("prep_act"), sem("prep_dve")
        dchain = sem("vector_chain")
        turn = [sem("top_turn"), sem("gather_turn")]
        qz_ready = [slot_sem(f"qz{g}_ready", g) for g in GS]
        sc_ready = [slot_sem(f"scores{g}_ready", g) for g in ("A", "B", "C")]
        nm_ready = [slot_sem(f"negmax{g}_ready", g) for g in ("A", "B", "C")]
        pr_ready = [slot_sem(f"probs{g}_ready", g) for g in ("A", "B", "C")]
        pt_ready = [slot_sem(f"probsT{g}_ready", g) for g in ("A", "B", "C")]
        ptsb_ready = [slot_sem(f"probsTcopy{g}_ready", g) for g in ("A", "B", "C")]
        av_ready = [slot_sem(f"av{g}_ready", g) for g in ("A", "B", "C")]
        wqs_ready = slot_sem("wqs_ready", "C")
        q_ready = slot_sem("q_ready", "C")
        qs_ready = slot_sem("qs_ready", "C")
        rc_ready = slot_sem("rowsum_recip_ready", "C")
        oc_ready = slot_sem("oc_ready", "C")
        oct_ready = slot_sem("ocT_ready", "C")
        octsb_ready = slot_sem("ocTcopy_ready", "C")
        wo_ready = slot_sem("wo_ready", "C")
        wo_used = slot_sem("wo_used", "C")
        sim_ready = slot_sem("sim_ready", "T")
        ng_ready = slot_sem("negtop_ready", "T")
        ew_ready = slot_sem("topexp_ready", "T")
        row_ready = slot_sem("rows_ready", "T")
        wt_ready = slot_sem("topweights_ready", "T")
        gathered = [sem(f"gathered{i}") for i in range(2)]
        gathered_last = [sem(f"gathered_last{i}") for i in range(2)]
        dg_ready = [sem(f"diag_half{i}_ready") for i in range(2)]
        sum_ready = sem("sums_ready")
        sumsb_ready = sem("sumcopy_ready")
        for q in (*dg_ready, sum_ready, sumsb_ready):
            starts.append((q, 2 * SLOTS + 2))
        th_ready = slot_sem("tanh_ready", "F")
        h1_ready = slot_sem("h1_ready", "F")
        sg_ready = slot_sem("tanh_half_ready", "F")
        h2_ready = slot_sem("h2_ready", "F")
        h2t_ready = slot_sem("h2T_ready", "F")
        h2tsb_ready = slot_sem("h2Tcopy_ready", "F")
        y_ready = slot_sem("y_ready", "F")
        f_ready = sem("h_ready")
        starts.append((f_ready, SLOTS * (1 + LAG["F"]) - 2))
        pe_done, act_done, dve_done = sem("pe_period"), sem("act_period"), sem("dve_period")
        g1_oT, g1_oTsb, g1_pr = (period_sem(f"bB_{n}", 5) for n in ("oT", "oTcopy", "proj"))
        c_xn, c_xT, c_xTsb, c_q, c_qsb = (period_sem(f"bC_{n}", 4) for n in ("xn", "xT", "xTcopy", "qkv", "qkvcopy"))
        t_cp = period_sem("bT_copy", 3)
        g0_oT, g0_oTsb, g0_pr, g0_xn, g0_xT, g0_xTsb = (
            period_sem(f"bA_{n}", 2) for n in ("oT", "oTcopy", "proj", "xn", "xT", "xTcopy"))
        i_xn, i_xT, i_xTsb, i_q, i_qsb = (period_sem(f"bI_{n}", 1) for n in ("xn", "xT", "xTcopy", "qkv", "qkvcopy"))
        i_v = period_sem("bI_v", 1)
        o_ready = period_sem("result_ready", 6)
        x_used = sem("xin_used")

        block = ctx.enter_context(nc.Block())

        def periods(eng, one):
            for p in range(1, 6):
                one(p, p)
            with eng.Fori(6, NB + 1) as p:
                one(p, 6)
            for p in range(NB + 1, LAST + 1):
                one(p, p)

        def slots(eng, p, like, slot):
            fl = {g for g in "ATCBF" if active(g, like)}
            for tile in range(TILES):
                w = active("T", like)
                wprev = active("T", like - 1)
                cuts = [(0, 2, w if tile else wprev), (2, 6, w), (6, 8, w)]
                if w and not wprev and tile == 0:
                    cuts[1:2] = [(2, 4, w), (4, 6, w)]
                for lo, hi, ws in cuts:
                    stages = set(fl)
                    if ws:
                        stages.add("W")
                    if tile == TILES - 1 and lo == 6:
                        stages.discard("F")
                    if not stages:
                        continue
                    if hi - lo > 2:
                        with eng.Fori(lo, hi, 2) as j:
                            for s in range(2):
                                slot(tile, s, j + s, p * SLOTS + tile * H + s + j, stages)
                    else:
                        for s in range(2):
                            slot(tile, s, lo + s, p * SLOTS + (tile * H + lo + s), stages)

        def snap(eng, v):
            return v if isinstance(v, int) else eng.snap(v)

        def across(v):
            return v.rearrange("(o n) -> o n", o=1).to_broadcast([P, v.shape[0]])

        def column(v):
            return v.rearrange("(p o) -> p o", o=1)

        pkq = G[0][0:DK, 0:8, :].rearrange("p a b -> p (a b)")
        pkk = G[1][0:DK, 0:8, :].rearrange("p a b -> p (a b)")
        LOADS = [(w0q[:], a["w0q"]), (w0k[:], a["w0k"]), (w0v[:], a["w0v"]), (w0o[:], a["w0o"]),
                 (w1q[:], a["w1q"]), (w1k[:], a["w1k"]), (w1v[:], a["w1v"]), (w1o[:], a["w1o"]),
                 (b0q[:], column(a["b0q"])), (b0k[:], column(a["b0k"])), (b0v[:], across(a["b0v"])),
                 (b0o[:], across(a["b0o"])), (we[:], across(a["we"])), (wcq[:], a["wcq"]),
                 (wco[:], a["wco"].rearrange("(h d) c -> d h c", d=D)), (wft, a["wft"]), (bf[:], across(a["bf"])),
                 (lnw[:], column(a["lnw"])), (lnb[:], column(a["lnb"])), (pkq, a["pkq"]), (pkk, a["pkk"])]

        @block.sync
        def _(sp):
            for q, v in starts:
                sp.sem_inc(q, v)
            for i, (dst, src) in enumerate(LOADS):
                sp.dma_start(dst, src).then_inc(ld_w, 16)

            def one(p, like):
                if active("A", like):
                    if like > 1:
                        sp.wait_ge(x_used, p - 1)
                    sp.dma_start(xin[:], x[bass.ds(p - 1, 1)].rearrange("b (t p) c -> p (b t) c", p=P)).then_inc(ld_x, 16)
                for t in range(TILES):
                    for g in range(2):
                        if active(GS[g], like):
                            first = 1 + LAG[GS[g]]
                            if t >= 2 or like > first:
                                if g == 0:
                                    sp.wait_ge(mask_ready[0], (p - first) * TILES + t - 1)
                                else:
                                    sp.wait_ge(nm_ready[1], p * SLOTS + (t - 1) * H)
                            sp.dma_start(adjt[g][t % 2][:], adj[bass.ds(p - first, 1), t * P:(t + 1) * P, :]
                                         .rearrange("b p k -> p (b k)")).then_inc(ld_adj[g][t % 2], 16)
                    if t == 0 and active("F", like - 1):
                        sp.wait_ge(o_ready, p)
                        sp.dma_start(out[bass.ds(p - 6, 1)].rearrange("b (t p) c -> p (b t) c", p=P), xf[:]).then_inc(stored, 16)
            periods(sp, one)
            sp.wait_ge(o_ready, LAST + 1)
            sp.dma_start(out[NB - 1].rearrange("(t p) c -> p t c", p=P), xf[:]).then_inc(stored, 16)
            sp.wait_ge(stored, 16 * NB)

        @block.gpsimd
        def _(gp):
            done = [0]

            def link(ins):
                done[0] += 1
                ins.then_inc(const_ready, 1)
                gp.wait_ge(const_ready, done[0])

            link(gp.memset(ident[:], 0.0))
            link(gp.affine_select(out=ident[:], in_=ident[:], compare_op=ALU.not_equal, fill=1.0, base=0,
                                  pattern=[[-1, P]], channel_multiplier=1))
            link(gp.tensor_copy(identh[:], ident[:]))
            link(gp.memset(causal[:], 0.0))
            link(gp.affine_select(out=causal[:], in_=causal[:], compare_op=ALU.is_ge, fill=NEG1, base=0,
                                  pattern=[[-1, P]], channel_multiplier=1))
            link(gp.memset(avg, 1.0 / P))
            link(gp.memset(hmask[:], 0.25))
            link(gp.affine_select(out=hmask[:], in_=hmask[:], compare_op=ALU.is_ge, fill=0.0, base=0,
                                  pattern=[[-HD, H]], channel_multiplier=1))
            link(gp.affine_select(out=hmask[:], in_=hmask[:], compare_op=ALU.is_ge, fill=0.0, base=HD - 1,
                                  pattern=[[HD, H]], channel_multiplier=-1))
            for h in range(H):
                link(gp.memset(hoff[:, h:h + 1], float(h * NKV)))
            for i in range(NC):
                link(gp.memset(iota[:, i:i + 1], float(i)))
            assert done[0] == NCONST
            gp.wait_ge(prep_pe, 1)

            def gather(m, s, signal):
                gp.wait_ge(row_ready, m + (1 + 2 * SLOTS))
                gp.wait_ge(sum_ready, m + (1 + 2 * SLOTS))
                gp.sem_inc(turn[1], 1)
                for j in range(TOPK):
                    gp.indirect_dma_start(out=G[s][:, j, :], out_offset=None, in_=a["table"][:, :],
                                          in_offset=bass.IndirectOffsetOnAxis(ap=row[s][:, j:j + 1], axis=0)
                                          ).then_inc(signal, 16)

            with gp.Fori(0, NB * SLOTS - 2, 2) as m:
                for s in range(2):
                    gather(m + s, s, gathered[s])
            for s in range(2):
                gather(NB * SLOTS - 2 + s, s, gathered_last[s])

        @block.tensor
        def _(pe):
            pe.wait_ge(ld_w, 16 * len(LOADS))
            pe.wait_ge(const_ready, NCONST)
            for i in range(2 * H):
                last = pe.matmul(bank[i // 4][:, (i % 4) * P:(i % 4 + 1) * P], pkq[:, i * P:(i + 1) * P],
                                 pkk[:, i * P:(i + 1) * P], start=True, stop=True)
            last.then_inc(prep_pe, 1)
            pe.wait_ge(prep_dve, 1)
            pe.matmul(bank[6][:, 0:P], avg, wf[:], start=True, stop=True)
            pe.matmul(bank[6][:, P:2 * P], hT[:, 0:P], wft, start=True, stop=True).then_inc(prep_pe, 1)
            pe.wait_ge(prep_act, 4)
            pe.wait_ge(prep_dve, 2)

            def transposes(dst, src, ready, n=TILES):
                for t in range(n):
                    last = pe.transpose(dst[:, t * P:(t + 1) * P], src[:, t * P:(t + 1) * P], ident[:])
                last.then_inc(ready, 1)

            def projection(dst, src, w, copied, proj, p):
                pe.wait_ge(copied, p)
                for t in range(TILES):
                    last = pe.matmul(dst[:, t * P:(t + 1) * P], src[:, t * P:(t + 1) * P], w[:], start=True, stop=True)
                last.then_inc(proj, 1)

            def qkv(banks, wq, wk, wv, src, ready):
                pe.matmul(banks[0][:], wq[:], src[:], start=True, stop=True)
                pe.matmul(banks[1][:], wk[:], src[:], start=True, stop=True)
                for t in range(TILES):
                    last = pe.matmul(banks[2][:, t * P:(t + 1) * P], src[:, t * P:(t + 1) * P], wv[:], start=True, stop=True)
                last.then_inc(ready, 1)

            def boundary(p, like):
                if like > 1:
                    pe.wait_ge(act_done, p - 1)
                    pe.wait_ge(dve_done, p - 1)
                if active("F", like - 1):
                    for q in (h2t_ready, y_ready):
                        pe.sem_inc(q, SLOTS - ITERS)
                if active("T", like - 1):
                    pe.wait_ge(sumsb_ready, p * SLOTS)
                if active("B", like - 1):
                    transposes(bank[0], oo[1][:].rearrange("p t c -> p (t c)"), g1_oT)
                if active("A", like - 1):
                    transposes(bank[2], oo[0][:].rearrange("p t c -> p (t c)"), g0_oT)
                if active("B", like - 1):
                    projection(bank[1], oTB, w1o, g1_oTsb, g1_pr, p)
                if active("A", like - 1):
                    projection(bank[3], oTA, w0o, g0_oTsb, g0_pr, p)
                if active("C", like - 1):
                    pe.wait_ge(c_xn, p)
                    transposes(bank[4], xnC, c_xT)
                if active("A", like):
                    pe.wait_ge(i_xn, p)
                    transposes(bank[0], xnI, i_xT)
                if active("C", like - 1):
                    pe.wait_ge(c_xTsb, p)
                    qkv(bank[5:8], w1q, w1k, w1v, xTC, c_q)
                if active("A", like):
                    pe.wait_ge(i_xTsb, p)
                    qkv((bank[0], bank[2], bank[4]), w0q, w0k, w0v, xTI, i_q)
                if active("A", like - 1):
                    pe.wait_ge(g0_xn, p)
                    transposes(bank[3], xnA, g0_xT)
                if active("C", like - 1):
                    pe.wait_ge(c_qsb, p)
                if active("A", like):
                    pe.wait_ge(i_qsb, p)
                    pe.wait_ge(i_v, p)
                if active("T", like):
                    pe.wait_ge(g0_xTsb, p)
                if active("C", like):
                    pe.wait_ge(t_cp, p)

            def slot(tile, s, h, n, st, p, like, cbase):
                v1 = snap(pe, n + 1)
                nk = (tile + 1) * P
                cur = slice(tile * P, (tile + 1) * P)

                def scores(g):
                    pe.wait_ge(qz_ready[g], v1)
                    pe.matmul(SC[g][:], qz[g][:], kT[g][:], start=True, stop=False)
                    pe.matmul(SC[g][:], identh[:], maskt[g][tile % 2][:], start=False, stop=True).then_inc(sc_ready[g], 1)

                def probs_T(g, cnt):
                    pe.wait_ge(pr_ready[g], v1)
                    transposes(SC[g], pr[g], pt_ready[g], cnt)

                def head_av(g):
                    pe.wait_ge(ptsb_ready[g], v1)
                    for kt in range(TILES):
                        last = pe.matmul(psO[g], prT[g][:, kt * P:(kt + 1) * P], vv[g][:, kt, bass.ds(h * HD, HD)],
                                         start=kt == 0, stop=kt == TILES - 1)
                    last.then_inc(av_ready[g], 1)

                def sums(lo, hi):
                    half = lo // 8
                    if lo == 0 and "T" in st:
                        pe.wait_ge(gathered[s], (n - s) * P - (2 * SLOTS + 2) * P + 256)
                    elif lo == 0:
                        pe.wait_ge(gathered_last[s], 16 * TOPK)
                    pe.wait_ge(dg_ready[half], v1)
                    for j in range(lo, hi):
                        pe.matmul(psK[s], G[s][:, j, 0:D], dg[s][:, j, :], start=j == 0, stop=j == TOPK - 1,
                                  skip_group_check=True)
                        last = pe.matmul(psV[s], dg[s][:, j, :], G[s][:, j, D:2 * D], start=False, stop=j == TOPK - 1,
                                         skip_group_check=True)
                    if hi == TOPK:
                        last.then_inc(sum_ready, 1)

                if s == 0:
                    for g in range(2):
                        if GS[g] in st:
                            pe.wait_ge(mask_ready[g], (p - 1 - LAG[GS[g]]) * TILES + tile + 1)
                if "A" in st:
                    scores(0)
                if "B" in st:
                    scores(1)
                if "C" in st:
                    pe.wait_ge(wqs_ready, v1)
                    pe.matmul(psq, wqs[:], xcT[:, cur], start=True, stop=True).then_inc(q_ready, 1)
                if "T" in st:
                    pe.matmul(psS, xtT[:, cur], simw[:, bass.ds(h, 1), :, :].rearrange("p a b c -> p (a b c)"),
                              start=True, stop=True).then_inc(sim_ready, 1)
                if "C" in st:
                    pe.wait_ge(qs_ready, v1)
                    kv = KT[:].rearrange("p (u c) -> p u c", c=P)
                    src = kv[:, bass.ds(cbase + h, tile * H + 1), :][:, 0:tile * H + 1:H, :] if tile else \
                        kv[:, bass.ds(cbase + h, 1), :]
                    pe.matmul(SC[2][:, 0:nk], qs[:], src, start=True, stop=False)
                    pe.matmul(SC[2][:, cur], identh[:], causal[:], start=False, stop=True).then_inc(sc_ready[2], 1)
                if "W" in st:
                    pe.wait_ge(sumsb_ready, n - 1)
                    sums(0, 8)
                if "A" in st:
                    probs_T(0, TILES)
                if "B" in st:
                    probs_T(1, TILES)
                if "F" in st:
                    pe.wait_ge(h2_ready, v1)
                    transposes(psH, h1[:].rearrange("p t c -> p (t c)"), h2t_ready)
                if "A" in st:
                    head_av(0)
                if "B" in st:
                    head_av(1)
                if "C" in st:
                    probs_T(2, tile + 1)
                if "F" in st:
                    pe.wait_ge(h2tsb_ready, v1)
                    for t in range(TILES):
                        last = pe.matmul(psY[:, t * P:(t + 1) * P], hT[:, t * P:(t + 1) * P], wf[:], start=True, stop=True)
                    last.then_inc(y_ready, 1)
                if "C" in st:
                    pe.wait_ge(ptsb_ready[2], v1)
                    for kt in range(tile + 1):
                        last = pe.matmul(psC, prT[2][:, kt * P:(kt + 1) * P], VV[:, bass.ds((cbase + kt * H + h) * P, P)],
                                         start=kt == 0, stop=kt == tile)
                    last.then_inc(av_ready[2], 1)
                if "W" in st:
                    sums(8, 13)
                if "C" in st:
                    pe.wait_ge(oc_ready, v1)
                    transposes(psCT, oc, oct_ready, 1)
                if "W" in st:
                    sums(13, TOPK)
                if "C" in st:
                    pe.wait_ge(octsb_ready, v1)
                    pe.wait_ge(wo_used, n)
                    if "F" in st:
                        pe.wait_ge(f_ready, v1)
                    pe.matmul(psw, ocT[:], wco[:, bass.ds(h, 1), :].rearrange("p a b -> p (a b)"),
                              start=True, stop=True).then_inc(wo_ready, 1)

            def one(p, like):
                boundary(p, like)
                cbase = snap(pe, ((p + 1) % 2) * SLOTS)
                slots(pe, p, like, lambda *v: slot(*v, p, like, cbase))
                pe.drain().then_inc(pe_done, 1)
            periods(pe, one)
            pe.wait_ge(act_done, LAST)
            pe.wait_ge(dve_done, LAST)

        @block.scalar
        def _(act):
            act.wait_ge(prep_pe, 1)
            sw = simw[:].rearrange("p h a k -> p a h k")
            for i in range(4):
                act.activation(sw[:, i // 2, 4 * (i % 2):4 * (i % 2) + 4, :],
                               bank[i][:].rearrange("p (h k) -> p h k", k=P), ACT.Copy).then_inc(prep_act, 1)

            def copy_sums(k, i):
                act.wait_ge(sum_ready, k + 1)
                u = snap(act, ((k - 2) % (2 * SLOTS)) * P)
                act.activation(KT[:, bass.ds(u, P)], psK[i], ACT.Copy)
                act.activation(VV[:, bass.ds(u, P)], psV[i], ACT.Copy).then_inc(sumsb_ready, 1)

            def boundary(p, like):
                if active("T", like - 1):
                    copy_sums(p * SLOTS - 1, 1)
                if like > 1:
                    act.wait_ge(pe_done, p - 1)
                    act.wait_ge(dve_done, p - 1)
                else:
                    act.wait_ge(prep_dve, 2)
                if active("F", like - 1):
                    for q in (th_ready, sg_ready, h2tsb_ready):
                        act.sem_inc(q, SLOTS - ITERS)
                if active("B", like - 1):
                    act.wait_ge(g1_oT, p)
                    act.activation(oTB[:], bank[0][:], ACT.Copy).then_inc(g1_oTsb, 1)
                if active("A", like - 1):
                    act.wait_ge(g0_oT, p)
                    act.activation(oTA[:], bank[2][:], ACT.Copy).then_inc(g0_oTsb, 1)
                if active("C", like):
                    act.activation(xcT[:], xtT[:], ACT.Copy).then_inc(t_cp, 1)
                if active("C", like - 1):
                    act.wait_ge(c_xT, p)
                    act.activation(xTC[:], bank[4][:], ACT.Copy).then_inc(c_xTsb, 1)
                if active("A", like):
                    act.wait_ge(i_xT, p)
                    act.activation(xTI[:], bank[0][:], ACT.Copy).then_inc(i_xTsb, 1)
                if active("C", like - 1):
                    act.wait_ge(c_q, p)
                    act.activation(qT[1][:], bank[5][:], ACT.Copy)
                    act.activation(kT[1][:], bank[6][:], ACT.Copy)
                    act.activation(vv[1][:].rearrange("p t c -> p (t c)"), bank[7][:], ACT.Copy).then_inc(c_qsb, 1)
                if active("A", like):
                    act.wait_ge(i_q, p)
                    act.activation(qT[0][:], bank[0][:], ACT.Identity, bias=b0q[:])
                    act.activation(kT[0][:], bank[2][:], ACT.Identity, bias=b0k[:]).then_inc(i_qsb, 1)
                if active("A", like - 1):
                    act.wait_ge(g0_xT, p)
                    if active("C", like):
                        act.wait_ge(t_cp, p)
                    act.activation(xtT[:], bank[3][:], ACT.Copy).then_inc(g0_xTsb, 1)

            def slot(tile, s, h, n, st, p, like):
                v1 = snap(act, n + 1)
                nk = (tile + 1) * P
                cur = slice(tile * P, (tile + 1) * P)

                def head_q(g):
                    act.activation(qz[g][:], qT[g][:, cur], ACT.Copy, scale=hmask[:, bass.ds(h, 1)]).then_inc(qz_ready[g], 1)

                def probs(g, cols):
                    act.wait_ge(nm_ready[g], v1)
                    src = pr[1][:] if g == 1 else SC[g][:, 0:cols]
                    act.activation(pr[g][:, 0:cols], src, ACT.Exp, bias=nm[g][:], accum_out=rs[g][:]).then_inc(pr_ready[g], 1)

                def copy_T(g, cols):
                    act.wait_ge(pt_ready[g], v1)
                    act.activation(prT[g][:, 0:cols], SC[g][:, 0:cols], ACT.Copy).then_inc(ptsb_ready[g], 1)

                def diags(half):
                    for j in range(half * 8, half * 8 + 8):
                        last = act.activation(dg[s][:, j, :], ident[:], ACT.Copy, scale=wt[s][:, j:j + 1])
                    last.then_inc(dg_ready[half], 1)

                if "A" in st:
                    head_q(0)
                if "B" in st:
                    head_q(1)
                if "C" in st:
                    act.activation(wqs[:], wcq[:, bass.ds(h * D, D)], ACT.Copy).then_inc(wqs_ready, 1)
                if "F" in st:
                    act.wait_ge(f_ready, n)
                    act.activation(sg[:], hh[:], ACT.Tanh).then_inc(th_ready, 1)
                if "W" in st and not (isinstance(h, int) and tile == 0 and h == (2 if like == 2 else 0)):
                    copy_sums(n - 1, 1 - s)
                if "W" in st:
                    act.wait_ge(wt_ready, n - 1)
                    act.wait_ge(sum_ready, n - 1)
                    diags(0)
                if "C" in st:
                    act.wait_ge(q_ready, v1)
                    act.activation(qs[:], psq, ACT.Copy, scale=float(D) ** -0.5).then_inc(qs_ready, 1)
                if "A" in st:
                    probs(0, S)
                if "B" in st:
                    probs(1, S)
                if "F" in st:
                    act.wait_ge(h1_ready, v1)
                    act.activation(sg[:], h1[:], ACT.Tanh, scale=0.5).then_inc(sg_ready, 1)
                if "A" in st:
                    copy_T(0, S)
                if "B" in st:
                    copy_T(1, S)
                if "C" in st:
                    probs(2, nk)
                if "F" in st:
                    act.wait_ge(h2t_ready, v1)
                    act.activation(hT[:], psH[:], ACT.Copy).then_inc(h2tsb_ready, 1)
                if "W" in st:
                    diags(1)
                if "C" in st:
                    copy_T(2, nk)
                if "T" in st:
                    act.wait_ge(ng_ready, v1)
                    act.activation(ew[:], fin[:], ACT.Exp, bias=negm[:], accum_out=tsum[:]).then_inc(ew_ready, 1)
                if "C" in st:
                    act.wait_ge(av_ready[2], v1)
                    act.wait_ge(rc_ready, v1)
                    act.activation(oc[:], psC, ACT.Copy, scale=rr[2][:]).then_inc(oc_ready, 1)
                if "W" in st and "T" not in st and s == 1:
                    copy_sums(n, s)
                if "C" in st:
                    act.wait_ge(oct_ready, v1)
                    act.activation(ocT[:], psCT, ACT.Copy).then_inc(octsb_ready, 1)

            def one(p, like):
                boundary(p, like)
                if active("A", like):
                    act.wait_ge(i_qsb, p)
                if active("B", like):
                    act.wait_ge(c_qsb, p)
                slots(act, p, like, lambda *v: slot(*v, p, like))
                act.drain().then_inc(act_done, 1)
            periods(act, one)

        @block.vector
        def _(dve):
            chain = [0]

            def put(ins):
                ins.then_inc(dchain, 1)
                chain[0] += 1
                return chain[0]

            def need(v):
                dve.wait_ge(dchain, v)

            def restart():
                if chain[0]:
                    dve.wait_ge(dchain, chain[0])
                dve.sem_clear(dchain)
                chain[0] = 0

            def rsqrt_steps(src, eps, w=TILES):
                v, y, b, c = (t[:, 0:w] for t in (va, ya, yb, yc))
                yield lambda: dve.tensor_scalar(v, src, eps, None, ALU.add)
                yield lambda: dve.tensor_scalar(b.bitcast(i32), v.bitcast(i32), 1, None, ALU.logical_shift_right)
                yield lambda: dve.tensor_scalar(y.bitcast(i32), b.bitcast(i32), -1.0, float(0x5f3759df), ALU.mult, ALU.add)
                for _ in range(3):
                    yield lambda: dve.tensor_tensor(b, y, y, ALU.mult)
                    yield lambda: dve.scalar_tensor_tensor(out=c, in0=b, scalar=-0.5, in1=v, op0=ALU.mult, op1=ALU.mult)
                    yield lambda: dve.scalar_tensor_tensor(out=y, in0=c, scalar=1.5, in1=y, op0=ALU.add, op1=ALU.mult)

            def layernorms(*jobs):
                n = TILES * len(jobs)
                for k in range(n):
                    a = put(dve.bn_stats(stats[:, k, :], jobs[k // TILES][1][:, k % TILES, :]))
                need(a)
                for k in range(n):
                    a = put(dve.bn_aggr(mv[:, k, :], stats[:, k, :]))
                need(a)
                for step in rsqrt_steps(mv[:, 0:n, 1], EPS, n):
                    need(put(step()))
                for k in range(n):
                    dst, src, ready = jobs[k // TILES]
                    last = dve.tensor_scalar(dst[:, k % TILES, :], src[:, k % TILES, :], mv[:, k, 0:1], ya[:, k:k + 1],
                                             ALU.subtract, ALU.mult)
                    if k % TILES == TILES - 1:
                        last.then_inc(ready, 1)

            dve.wait_ge(ld_w, 16 * len(LOADS))
            dve.wait_ge(const_ready, NCONST)
            need(put(dve.memset(hT[:, P:2 * P], 1.0)))
            dve.tensor_scalar(hT[:, 0:P], hT[:, P:2 * P], lnb[:], None, ALU.mult)
            dve.tensor_scalar(wf[:], wft, lnw[:], None, ALU.mult).then_inc(prep_dve, 1)
            dve.wait_ge(prep_pe, 2)
            dve.tensor_tensor(wf[:], wf[:], bank[6][:, 0:P], ALU.subtract)
            dve.tensor_tensor(bf[:], bf[:], bank[6][:, P:2 * P], ALU.add).then_inc(prep_dve, 1)

            def add_head(tile, n):
                dve.wait_ge(wo_ready, n)
                dve.tensor_tensor(xc[:, tile, :], psw, xc[:, tile, :], ALU.add).then_inc(wo_used, 1)

            def boundary(p, like):
                restart()
                if like > 1:
                    dve.wait_ge(pe_done, p - 1)
                    dve.wait_ge(act_done, p - 1)
                if active("F", like - 1):
                    for q in (h1_ready, h2_ready):
                        dve.sem_inc(q, SLOTS - ITERS)
                    dve.tensor_tensor(xf[:], xf[:], hh[:], ALU.add).then_inc(o_ready, 1)
                if active("C", like - 1):
                    add_head(TILES - 1, p * SLOTS)
                if active("A", like):
                    dve.wait_ge(ld_x, p * 16)
                if active("C", like - 1):
                    dve.wait_ge(wo_used, p * SLOTS)
                    jobs = [(tokens(xnC), xc, c_xn)]
                else:
                    jobs = []
                if active("A", like):
                    jobs.append((tokens(xnI), xin, i_xn))
                if jobs:
                    layernorms(*jobs)
                jobs = []
                if active("B", like - 1):
                    dve.wait_ge(g1_pr, p)
                    if active("F", like - 1):
                        dve.wait_ge(stored, (p - 5) * 16)
                    need(put(dve.tensor_tensor(xf[:].rearrange("p t c -> p (t c)"), bank[1][:],
                                               xg[:].rearrange("p t c -> p (t c)"), ALU.add)))
                    dve.sem_inc(f_ready, 1)
                    jobs.append((hh, xf, f_ready))
                if active("A", like - 1):
                    dve.wait_ge(g0_pr, p)
                if active("C", like - 1):
                    need(put(dve.tensor_copy(xg[:], xc[:])))
                if active("C", like):
                    need(put(dve.tensor_copy(xc[:], xa[:])))
                if active("A", like - 1):
                    need(put(dve.tensor_tensor(xa[:].rearrange("p t c -> p (t c)"), bank[3][:],
                                               x0[:].rearrange("p t c -> p (t c)"), ALU.add)))
                    put(dve.tensor_tensor(xa[:], xa[:], b0o[:].rearrange("p (a c) -> p a c", a=1)
                                          .to_broadcast([P, TILES, D]), ALU.add))
                    jobs.append((tokens(xnA), xa, g0_xn))
                if active("A", like):
                    dve.tensor_copy(x0[:], xin[:]).then_inc(x_used, 1)
                if jobs:
                    need(chain[0])
                    layernorms(*jobs)
                if active("A", like):
                    dve.wait_ge(i_q, p)
                    dve.tensor_tensor(vv[0][:], bank[4][:].rearrange("p (t c) -> p t c", t=TILES),
                                      b0v[:].rearrange("p (a c) -> p a c", a=1).to_broadcast([P, TILES, D]),
                                      ALU.add).then_inc(i_v, 1)

            def masks(p, like, t):
                for g in range(2):
                    if active(GS[g], like):
                        first = 1 + LAG[GS[g]]
                        dve.wait_ge(ld_adj[g][t % 2], (p - first) * 32 + (t // 2 + 1) * 16)
                        dve.tensor_scalar(maskt[g][t % 2][:], adjt[g][t % 2][:], 0.0, (NEG0, NEG1)[g],
                                          (ALU.is_le, ALU.is_equal)[g], ALU.mult).then_inc(mask_ready[g], 1)

            def slot(tile, s, h, n, st, p, like):
                v1 = snap(dve, n + 1)
                nk = (tile + 1) * P
                restart()

                def negmax(g, src):
                    dve.tensor_reduce(nm[g][:], src, AX, ALU.max, negate=True).then_inc(nm_ready[g], 1)

                if "F" in st:
                    dve.wait_ge(th_ready, v1)
                    dve.scalar_tensor_tensor(out=h1[:], in0=sg[:], scalar=0.01, in1=hh[:], op0=ALU.mult,
                                             op1=ALU.add).then_inc(h1_ready, 1)
                if "A" in st:
                    dve.wait_ge(sc_ready[0], v1)
                    negmax(0, SC[0][:])
                if "B" in st:
                    dve.wait_ge(sc_ready[1], v1)
                    c = put(dve.scalar_tensor_tensor(out=pr[1][:], in0=adjt[1][tile % 2][:], scalar=we[:, bass.ds(h, 1)],
                                                     in1=SC[1][:], op0=ALU.mult, op1=ALU.add))
                if "T" in st:
                    dve.wait_ge(sim_ready, v1)
                    dve.sem_inc(turn[0], 1)
                    a0 = put(dve.max(top[:, 0, 0:8], psS[:, 0:128]))
                    a1 = put(dve.max(top[:, 1, 0:8], psS[:, 128:256]))
                if "B" in st:
                    need(c)
                    negmax(1, pr[1][:])
                if "T" in st:
                    need(a1)
                    a0 = put(dve.match_replace(rest[:, 0, :], top[:, 0, 0:8], psS[:, 0:128], LOW))
                    a1 = put(dve.match_replace(rest[:, 1, :], top[:, 1, 0:8], psS[:, 128:256], LOW))
                    dve.max_index(topi[:, 0, 0:8], top[:, 0, 0:8], psS[:, 0:128])
                    dve.max_index(topi[:, 1, 0:8], top[:, 1, 0:8], psS[:, 128:256])
                    need(a1)
                    a0 = put(dve.max(top[:, 0, 8:16], rest[:, 0, :]))
                    a1 = put(dve.max(top[:, 1, 8:16], rest[:, 1, :]))
                if "C" in st:
                    dve.wait_ge(sc_ready[2], v1)
                    negmax(2, SC[2][:, 0:nk])
                if "T" in st:
                    need(a1)
                    dve.max_index(topi[:, 0, 8:16], top[:, 0, 8:16], rest[:, 0, :])
                    ai = put(dve.max_index(topi[:, 1, 8:16], top[:, 1, 8:16], rest[:, 1, :]))
                if "C" in st and not (tile == 0 and isinstance(h, int) and h == 0):
                    add_head(tile - 1 if isinstance(h, int) and h == 0 else tile, n)
                if "F" in st:
                    dve.wait_ge(sg_ready, v1)
                    dve.scalar_tensor_tensor(out=h1[:], in0=sg[:], scalar=1.0, in1=h1[:], op0=ALU.add,
                                             op1=ALU.mult).then_inc(h2_ready, 1)
                if "T" in st:
                    need(ai)
                    at = 0
                    for i0, r, c in GROUPS:
                        def grid(t, k):
                            v = t[:, 0, i0:i0 + r].rearrange("p (r c) -> p r c", c=1).to_broadcast([P, r, c]) if k == 0 else \
                                t[:, 1, 0:c].rearrange("p (r c) -> p r c", r=1).to_broadcast([P, r, c])
                            return v
                        dst = slice(at, at + r * c)
                        dve.tensor_tensor(cand[:, dst].rearrange("p (r c) -> p r c", c=c), grid(top, 0), grid(top, 1), ALU.add)
                        ac = put(dve.scalar_tensor_tensor(out=candi[:, dst].rearrange("p (r c) -> p r c", c=c), in0=grid(topi, 1),
                                                          scalar=float(NKEYS), in1=grid(topi, 0), op0=ALU.mult, op1=ALU.add))
                        at += r * c
                if "F" in st:
                    dve.wait_ge(h2_ready, v1)
                    for t in range(TILES):
                        a = put(dve.bn_stats(stats[:, t, :], h1[:, t, :]))
                newton = []
                if "F" in st:
                    need(a)
                    for t in range(TILES):
                        a = put(dve.bn_aggr(mv[:, t, :], stats[:, t, :]))
                    newton = list(rsqrt_steps(mv[:, 0:TILES, 1], 4 * EPS))
                    nw = [a]

                def newton_step(k=1):
                    for _ in range(k):
                        if newton:
                            need(nw[0])
                            nw[0] = put(newton.pop(0)())

                newton_step()
                if "T" in st:
                    need(ac)
                    b = put(dve.max(fin[:, 0:8], cand[:]))
                    newton_step()
                    need(b)
                    dve.max_index(pos[:, 0:8], fin[:, 0:8], cand[:])
                    b = put(dve.match_replace(candr[:], fin[:, 0:8], cand[:], LOW))
                    newton_step()
                    need(b)
                    b = put(dve.max(fin[:, 8:16], candr[:]))
                    newton_step()
                    need(b)
                    dve.tensor_scalar(negm[:], fin[:, 0:1], -1.0, None, ALU.mult).then_inc(ng_ready, 1)
                    b = put(dve.max_index(pos[:, 8:16], fin[:, 8:16], candr[:]))
                newton_step(20)
                for g in range(3):
                    if "ABC"[g] in st:
                        dve.wait_ge(pr_ready[g], v1)
                        r = dve.reciprocal(rr[g][:], rs[g][:])
                        if g == 2:
                            r.then_inc(rc_ready, 1)
                        else:
                            lr = put(r)
                if "T" in st:
                    need(b)
                    b = put(dve.tensor_tensor(hit[:], pos[:].rearrange("p (j c) -> p j c", c=1).to_broadcast([P, TOPK, NC]),
                                              iota[:].rearrange("p (j c) -> p j c", j=1).to_broadcast([P, TOPK, NC]), ALU.is_equal))
                for g in range(2):
                    if GS[g] in st:
                        dve.wait_ge(av_ready[1 if "B" in st else 0], v1)
                        need(lr)
                        dve.tensor_scalar(oo[g][:, tile, bass.ds(h * HD, HD)], psO[g], rr[g][:], None, ALU.mult)
                if "T" in st:
                    need(b)
                    b = put(dve.tensor_tensor(hit[:], hit[:], candi[:].rearrange("p (j c) -> p j c", j=1)
                                              .to_broadcast([P, TOPK, NC]), ALU.mult))
                if "F" in st:
                    dve.wait_ge(y_ready, v1)
                    need(nw[0])
                    for t in range(TILES):
                        last = dve.scalar_tensor_tensor(out=hh[:, t, :], in0=psY[:, t * P:(t + 1) * P], scalar=ya[:, t:t + 1],
                                                        in1=bf[:], op0=ALU.mult, op1=ALU.add)
                    last.then_inc(f_ready, 1)
                if "T" in st:
                    need(b)
                    b = put(dve.tensor_reduce(rowf[:], hit[:], AX, ALU.add))
                    dve.wait_ge(ew_ready, v1)
                    b2 = put(dve.reciprocal(trec[:], tsum[:]))
                    if not (like == 2 and tile == 0 and isinstance(h, int) and h < 2):
                        dve.wait_ge(gathered[s], (n - s) * P - (2 * SLOTS + 2) * P + 256)
                        dve.wait_ge(dg_ready[1], v1)
                    need(b)
                    dve.tensor_scalar(row[s][:], rowf[:], hoff[:, bass.ds(h, 1)], None, ALU.add).then_inc(row_ready, 1)
                    need(b2)
                    dve.tensor_scalar(wt[s][:], ew[:], trec[:], None, ALU.mult).then_inc(wt_ready, 1)

            def one(p, like):
                boundary(p, like)
                at = [-1]

                def tile_slot(tile, *v):
                    if tile != at[0]:
                        at[0] = tile
                        masks(p, like, tile)
                    slot(tile, *v, p, like)

                slots(dve, p, like, tile_slot)
                dve.drain().then_inc(dve_done, 1)

            periods(dve, one)
            dve.wait_ge(act_done, LAST)
            dve.tensor_tensor(xf[:], xf[:], hh[:], ALU.add).then_inc(o_ready, 1)


def kernel(**i):
    import concourse.bacc as bacc
    from concourse.bass_utils import run_bass_kernel_spmd

    i = {k: np.asarray(v) for k, v in i.items()}
    arrays = dict(
        x=i["x"], adj=i["adj"],
        w0q=i["L0_gnn_Wq"], w0k=i["L0_gnn_Wk"], w0v=i["L0_gnn_Wv"], w0o=i["L0_gnn_Wo"],
        b0q=i["L0_gnn_bq"], b0k=i["L0_gnn_bk"], b0v=i["L0_gnn_bv"], b0o=i["L0_gnn_bo"],
        pkq=i["L0_ffn_Wq_pk"].reshape(D, 2 * H, DK).transpose(2, 1, 0).reshape(DK, 2 * H * D),
        pkk=i["L0_ffn_pk_keys"].transpose(3, 0, 2, 1).reshape(DK, 2 * H * NKEYS),
        wcq=i["L0_ffn_Wq"], wco=i["L0_ffn_Wo"],
        table=np.concatenate([i["L0_ffn_keys_table"], i["L0_ffn_values_table"]], axis=1),
        w1q=i["L1_gnn_W_q"].T, w1k=i["L1_gnn_W_k"].T, w1v=i["L1_gnn_W_v"].T, w1o=i["L1_gnn_W_o"].T,
        we=i["L1_gnn_W_e"].reshape(H), lnw=i["L1_ffn_ln_w"], lnb=i["L1_ffn_ln_b"],
        wft=i["L1_ffn_W"].T, bf=i["L1_ffn_b"])
    nc = bacc.Bacc("TRN2", target_bir_lowering=False, num_devices=1)
    feeds, args = {}, {}
    for name, v in arrays.items():
        v = np.ascontiguousarray(v)
        feeds[f"in_{name}"] = v
        args[name] = nc.dram_tensor(f"in_{name}", v.shape, mybir.dt.from_np(v.dtype), kind="ExternalInput").ap()
    out = nc.dram_tensor("out_y", (NB, S, D), mybir.dt.float32, kind="ExternalOutput").ap()
    build(nc, args, out)
    r = run_bass_kernel_spmd(nc, [feeds], core_ids=[0])
    return r.results[0]["out_y"]
```
